# Optimizing a Trainium2 kernel written in Bass

```python
import numpy as np
import jax
import jax.numpy as jnp

def _softmax(x, axis=-1):
    return jax.nn.softmax(x, axis=axis)

def _gelu(x):
    return jax.nn.gelu(x, approximate=True)

def _silu(x):
    return jax.nn.silu(x)

def _sigmoid(x):
    return jax.nn.sigmoid(x)

def _layernorm(x, axis=-1, eps=1e-05):
    m = jnp.mean(x, axis=axis, keepdims=True)
    v = jnp.var(x, axis=axis, keepdims=True)
    return (x - m) / jnp.sqrt(v + eps)

def _scatter_add(tgt, idx, src, axis=0):
    return tgt.at[idx].add(src)

def _segment_sum(src, seg, n):
    return jax.ops.segment_sum(src, seg, n)
kernel_name = 'mk_adj_resnorm_d2_adj_r2_cee71b'

def setup_inputs(seed: int=0):
    np.random.seed(seed)
    _w = jnp.asarray

    def _rec_inputs():
        import jax
        import jax.numpy as jnp
        _gk = jax.random.key(seed)
        x = -0.0002928 + 1 * jax.random.normal(jax.random.fold_in(_gk, 1), (128, 64, 256), jnp.float32)
        _w = (1.0 + jnp.arange(64, dtype=jnp.float32)) ** (-0.5)
        _w = _w / _w.mean()
        _pij = jnp.clip(0.0625 * _w[:, None] * _w[None, :], 0.0, 1.0)
        _a = jax.random.uniform(jax.random.fold_in(_gk, 2), (128, 64, 64)) < _pij
        adj = _a.astype(jnp.int32)
        return (x, adj)
    x, adj = _rec_inputs()

    def _L0_gnn_setup():
        import jax, jax.numpy as jnp
        import numpy as np
        L = 3
        D = 256
        B, N = (8, 512)
        EPS = 1e-05

        def layernorm(x, gamma, beta):
            mu = jnp.mean(x, axis=-1, keepdims=True)
            var = jnp.var(x, axis=-1, keepdims=True)
            return (x - mu) * jax.lax.rsqrt(var + EPS) * gamma + beta
        key = jax.random.key(seed)
        ks = jax.random.split(key, 12)
        s = 1.0 / np.sqrt(D)
        node_features = jax.random.normal(ks[0], (B, N, D), dtype=jnp.float32)
        adjacency_matrix = jax.random.randint(ks[1], (B, N, N), 0, 2, dtype=jnp.int32)
        return {'node_features': node_features, 'adjacency_matrix': adjacency_matrix, 'attn_w': jax.random.normal(ks[2], (L, 2 * D), dtype=jnp.float32) * (1.0 / np.sqrt(2 * D)), 'attn_b': jax.random.normal(ks[3], (L,), dtype=jnp.float32) * 0.01, 'W1': jax.random.normal(ks[4], (L, D, 4 * D), dtype=jnp.float32) * s, 'b1': jnp.zeros((L, 4 * D), dtype=jnp.float32), 'W2': jax.random.normal(ks[5], (L, 4 * D, D), dtype=jnp.float32) * (1.0 / np.sqrt(4 * D)), 'b2': jnp.zeros((L, D), dtype=jnp.float32), 'g1': jnp.ones((L, D), dtype=jnp.float32), 'beta1': jnp.zeros((L, D), dtype=jnp.float32), 'g2': jnp.ones((L, D), dtype=jnp.float32), 'beta2': jnp.zeros((L, D), dtype=jnp.float32)}
    _L0_gnn_all = _L0_gnn_setup()
    _L0_gnn_in = {k: v for k, v in _L0_gnn_all.items() if k in ('attn_w', 'attn_b', 'W1', 'b1', 'W2', 'b2', 'g1', 'beta1', 'g2', 'beta2')}
    del _L0_gnn_all

    def _L1_gnn_setup():
        import jax, jax.numpy as jnp
        import numpy as np
        ALPHA = 0.2

        def _leaky(x):
            return jnp.where(x >= 0, x, ALPHA * x)
        key = jax.random.key(seed)
        k1, k2, k3, k4 = jax.random.split(key, 4)
        B, N, F_in, F_out = (4, 1024, 256, 256)
        h = jax.random.normal(k1, (B, N, F_in), dtype=jnp.float32)
        W = jax.random.normal(k2, (F_in, F_out), dtype=jnp.float32) * 0.05
        a = jax.random.normal(k3, (2 * F_out, 1), dtype=jnp.float32) * 0.05
        adj = jax.random.randint(k4, (B, N, N), 0, 2, dtype=jnp.int32)
        return {'h': h, 'W': W, 'a': a, 'adj': adj}
    _L1_gnn_all = _L1_gnn_setup()
    _L1_gnn_in = {k: v for k, v in _L1_gnn_all.items() if k in ('W', 'a')}
    del _L1_gnn_all
    return {'x': x, 'adj': adj, 'L0_gnn_attn_w': _L0_gnn_in['attn_w'], 'L0_gnn_attn_b': _L0_gnn_in['attn_b'], 'L0_gnn_W1': _L0_gnn_in['W1'], 'L0_gnn_b1': _L0_gnn_in['b1'], 'L0_gnn_W2': _L0_gnn_in['W2'], 'L0_gnn_b2': _L0_gnn_in['b2'], 'L0_gnn_g1': _L0_gnn_in['g1'], 'L0_gnn_beta1': _L0_gnn_in['beta1'], 'L0_gnn_g2': _L0_gnn_in['g2'], 'L0_gnn_beta2': _L0_gnn_in['beta2'], 'L1_gnn_W': _L1_gnn_in['W'], 'L1_gnn_a': _L1_gnn_in['a']}

def reference(x, adj, L0_gnn_attn_w, L0_gnn_attn_b, L0_gnn_W1, L0_gnn_b1, L0_gnn_W2, L0_gnn_b2, L0_gnn_g1, L0_gnn_beta1, L0_gnn_g2, L0_gnn_beta2, L1_gnn_W, L1_gnn_a):
    import jax
    import jax.numpy as jnp

    def _L0_gnn_ref(node_features, adjacency_matrix, attn_w, attn_b, W1, b1, W2, b2, g1, beta1, g2, beta2):
        import jax, jax.numpy as jnp
        import numpy as np
        L = 3
        D = 256
        B, N = (8, 512)
        EPS = 1e-05

        def layernorm(x, gamma, beta):
            mu = jnp.mean(x, axis=-1, keepdims=True)
            var = jnp.var(x, axis=-1, keepdims=True)
            return (x - mu) * jax.lax.rsqrt(var + EPS) * gamma + beta
        n = adjacency_matrix.shape[-1]
        mask = adjacency_matrix.astype(jnp.float32) + jnp.eye(n, dtype=jnp.float32) > 0
        x = node_features
        d = x.shape[-1]
        for l in range(attn_w.shape[0]):
            si = x @ attn_w[l, :d]
            sj = x @ attn_w[l, d:]
            scores = si[:, :, None] + sj[:, None, :] + attn_b[l]
            scores = jnp.where(scores >= 0, scores, 0.2 * scores)
            scores = jnp.where(mask, scores, -jnp.inf)
            attn = jax.nn.softmax(scores, axis=-1)
            agg = jnp.einsum('bij,bjd->bid', attn, x)
            h = layernorm(x + agg, g1[l], beta1[l])
            ff = jax.nn.gelu(h @ W1[l] + b1[l], approximate=False) @ W2[l] + b2[l]
            x = layernorm(h + ff, g2[l], beta2[l])
        return x

    def _L1_gnn_ref(h, W, a, adj):
        import jax, jax.numpy as jnp
        import numpy as np
        ALPHA = 0.2

        def _leaky(x):
            return jnp.where(x >= 0, x, ALPHA * x)
        F_out = W.shape[1]
        Wh = jnp.matmul(h, W)
        Wh_sg = jax.lax.stop_gradient(Wh)
        a1 = a[:F_out, 0]
        a2 = a[F_out:, 0]
        s_i = Wh_sg @ a1
        s_j = Wh_sg @ a2
        e = _leaky(s_i[:, :, None] + s_j[:, None, :])
        e = jnp.where(adj > 0, e, jnp.float32(-9000000000000000.0))
        attention = jax.nn.softmax(e, axis=1)
        h_prime = jnp.einsum('bij,bjf->bif', attention, Wh)
        return _leaky(h_prime)
    x = _layernorm(x + _L0_gnn_ref(x, adj, L0_gnn_attn_w, L0_gnn_attn_b, L0_gnn_W1, L0_gnn_b1, L0_gnn_W2, L0_gnn_b2, L0_gnn_g1, L0_gnn_beta1, L0_gnn_g2, L0_gnn_beta2), axis=-1)
    x = _layernorm(x + _L1_gnn_ref(x, L1_gnn_W, L1_gnn_a, adj), axis=-1)
    return x

_drawn_inputs = setup_inputs


def setup_inputs(seed=0):
    import zlib

    import numpy as np

    out = dict(_drawn_inputs(seed))
    spreads = {'L0_gnn_b1': (0.0, 0.1),
     'L0_gnn_b2': (0.0, 0.1),
     'L0_gnn_g1': (1.0, 0.2),
     'L0_gnn_beta1': (0.0, 0.1),
     'L0_gnn_g2': (1.0, 0.2),
     'L0_gnn_beta2': (0.0, 0.1)}
    factors = {'L0_gnn_attn_b': 64.0}
    for name, (base, spread) in spreads.items():
        noise = np.random.default_rng([zlib.crc32(name.encode()), seed]).standard_normal(out[name].shape)
        drawn = base * np.exp(spread * noise) if base else spread * noise
        out[name] = jnp.asarray(drawn.astype(out[name].dtype))
    for name, factor in factors.items():
        out[name] = (out[name] * factor).astype(out[name].dtype)
    return out
```

```python
from contextlib import ExitStack

import concourse.bass as bass
from concourse import mybir

F32 = mybir.dt.float32
F32R = mybir.dt.float32r
BF16 = mybir.dt.bfloat16
I32 = mybir.dt.int32
ALU = mybir.AluOpType
ACT = mybir.ActivationFunctionType
AX = mybir.AxisListType

P = 128
T = 4
BUFS = 4
LAYERS = 3
ROUND = BUFS * LAYERS
U_BUFS = 3
FIRST = 3
EPS = 1e-5
SLOPE = 0.2
OFF = -3.0e38
GAT_OFF = -9.0e15


def layer_of(s):
    return (s % ROUND) // BUFS


def buf_of(s):
    return s % BUFS


def u_of(s):
    return buf_of(s) % U_BUFS


def group_of(r, s):
    return r * BUFS + (BUFS * (s // ROUND) + s % BUFS)


def upto(r, s, per=1, part=None):
    return r * (ROUND * per) + (s * per + (per if part is None else part))


def upto_gat(r, s, per=1, part=None):
    return r * (BUFS * per) + ((BUFS * (s // ROUND) + s % BUFS) * per + (per if part is None else part))


class Slot:

    def __init__(self, r, s, rounds):
        q = (r if isinstance(r, int) else 1) * ROUND + s
        jobs = rounds * ROUND
        self.r, self.s = r, s
        self.mlp = s if 0 <= q < jobs else None
        self.norm = s - 1 if 0 <= q - 1 < jobs else None
        self.score = s + 2 if 0 <= q + 2 < jobs else None
        self.mix = s + 1 if 0 <= q + 1 < jobs else None

        def last_layer(d):
            return s - d if 0 <= q - d < jobs and layer_of(s - d) == LAYERS - 1 else None

        self.gat_sum = last_layer(1)
        self.gat_a = last_layer(2)
        self.gat_b = last_layer(3)
        self.fresh = self.score if self.score is not None and layer_of(self.score) == 0 else None
        self.starting = s < 1 and isinstance(r, int) and r == 0


def graph_net_kernel(nc, x, adj, attn_w, attn_b, W1, b1, W2, b2, g1, beta1, g2, beta2, gat_W, gat_a, out):
    graphs, nodes, D = x.shape
    F = W1.shape[2]
    KD = D // P
    M = F // P
    per_tile = P // nodes
    groups = graphs // (per_tile * T)
    rounds = groups // BUFS
    NT = T * P
    assert groups % BUFS == 0 and nodes * per_tile == P and D * 2 == NT

    x_g = x.rearrange("(G t g) i d -> G (g i) t d", t=T, g=per_tile)
    adj_g = adj.rearrange("(G t g) i j -> G (g i) t j", t=T, g=per_tile)
    out_g = out.rearrange("(G t g) i d -> G (g i) t d", t=T, g=per_tile)

    with ExitStack() as ctx:
        def sb(name, shape, dt=F32):
            return ctx.enter_context(nc.sbuf_tensor(name, shape, dt))

        def ps(name, shape, dt=F32):
            return ctx.enter_context(nc.psum_tensor(name, shape, dt))

        def sem(name):
            return ctx.enter_context(nc.semaphore(name))

        w1h = sb("w1h", [P, LAYERS, KD, F], F32R)
        w1l = sb("w1l", [P, LAYERS, KD, F], F32R)
        w2h = sb("w2h", [P, LAYERS, M, D], F32R)
        w2l = sb("w2l", [P, LAYERS, M, D], F32R)
        gw = sb("gw", [P, KD, D])
        NCOL = LAYERS * (M + 2 * KD)
        col_rows = sb("col_rows", [NCOL, P])
        cols = sb("cols", [P, NCOL])
        score_w = sb("score_w", [P, LAYERS, 2 * D])
        gat_w = sb("gat_w", [P, 2 * D])
        score_b = sb("score_b", [P, LAYERS])
        g1_row = sb("g1_row", [P, LAYERS, D])
        hb_row = sb("hb_row", [P, LAYERS, D])
        g2_row = sb("g2_row", [P, LAYERS, D])
        be2_row = sb("be2_row", [P, LAYERS, D])
        ident = sb("ident", [P, P])
        ident_b = sb("ident_b", [P, P], BF16)
        eye = sb("eye", [P, nodes])
        gat_off = sb("gat_off", [P, P])
        half = sb("half", [P, T])
        xb = sb("xb", [P, BUFS, T, D])
        ht32 = sb("ht32", [P, KD, NT])
        hth = sb("hth", [P, 2, KD, NT], F32R)
        htl = sb("htl", [P, 2, KD, NT], F32R)
        gt = sb("gt", [P, 2, NT])
        gh = sb("gh", [P, 4, NT], F32R)
        gl = sb("gl", [P, 4, NT], F32R)
        adj_a = sb("adj_a", [P, T, nodes], I32)
        adj_e = sb("adj_e", [P, T, nodes])
        mask = sb("mask", [P, BUFS, T, P], BF16)
        sc = sb("sc", [P, 2 * T])
        sp = sb("sp", [P, T, P])
        pt = sb("pt", [P, T, P])
        unread = sb("unread", [P, 2 * T, D], BF16)
        mx = sb("mx", [P, T])
        nm = sb("nm", [P, T])
        rs = sb("rs", [P, T])
        ri = sb("ri", [P, T])
        norm_names = ("mix", "mlp", "u", "out")
        st = {n: sb(f"st_{n}", [P, T, 6]) for n in norm_names}
        mv = {n: sb(f"mv_{n}", [P, T, 2]) for n in norm_names}
        ve = {n: sb(f"ve_{n}", [P, T]) for n in norm_names}
        rd = {n: sb(f"rd_{n}", [P, T]) for n in norm_names}
        xr = sb("xr", [P, T, D])
        u = sb("u", [P, U_BUFS, T, D])
        whut = sb("whut", [P, 2, NT * KD])
        wh = whut[:, 0, :].rearrange("p (t d) -> p t d", t=T)
        ut = whut[:, 1, :].rearrange("p (k n) -> p k n", k=KD)
        adj_t = sb("adj_t", [P, T, nodes], I32)
        m01 = sb("m01", [P, T, P], BF16)
        gm = sb("gm", [P, T, P], BF16)
        ga = sb("ga", [P, T, P])
        gsc = sb("gsc", [P, 2 * T])
        gsp = sb("gsp", [P, T, P])
        gmx = sb("gmx", [P, T])
        gnm = sb("gnm", [P, T])
        grs = sb("grs", [P, T])
        gri = sb("gri", [P, T])
        stage = [u[:, 0:2, :, :].rearrange("p a t d -> p (a t d)"), whut[:, :, :].rearrange("p a n -> p (a n)")]
        beta_tmp = xr[:, 0:LAYERS, :]

        hid = ps("hid", [P, 2, NT])
        ff = ps("ff", [P, T, D])
        big = ps("big", [P, T * D])
        spread = ps("spread", [P, T, P])
        turn = ps("turn", [P, T, P])
        big_t = big[:, :].rearrange("p (t d) -> p t d", t=T)
        big_k = big[:, :].rearrange("p (k n) -> p k n", k=KD)
        turn_b = turn[:, :, :].rearrange("p t n -> p (t n)").bitcast(BF16)[:, 0:T * P].rearrange(
            "p (t n) -> p t n", t=T)

        names = """col_rows_in rows_in beta_in gw_in
            adj_a_in adj_t_in xr_in ident_ready consts_ready mask_ready0 cols_turned cols_ready hb_ready
            split_hi split_lo mask_edges mask_ready
            scores_in spread_done scores_sum scores_leaky max_done negmax exp_done probs_turned
            probs_ready sum_inverse mix_done mix_added z_turned ht_ready htl_ready h_scaled h_ready
            hid_done gelu_done gl_ready mlp2_done ff_done ff_added x_scaled x_ready
            u_part u_added ut_turned ut_ready wh_done wh_ready m01_ready masks_turned gm_ready ga_ready
            gscores_in gspread_done gscores_sum gleaky gmasked gmax_done gnegmax gexp_done gsum_inverse
            gprobs gmix_done gmix_scaled gmix_leaky out_added""".split()
        S = {n: sem(n) for n in names}
        x_in = [sem(f"x_in{i}") for i in range(BUFS)]
        w_in = [sem(f"w_in{i}") for i in range(2)]
        out_in = [sem(f"out_stored{i}") for i in range(U_BUFS)]
        stats_done = {n: sem(f"stats_{n}") for n in norm_names}
        mean_done = {n: sem(f"mean_{n}") for n in norm_names}
        var_ready = {n: sem(f"var_{n}") for n in norm_names}
        dev_ready = {n: sem(f"dev_{n}") for n in norm_names}
        normed = {n: sem(f"normed_{n}") for n in norm_names}

        N_SPLITS = 2 * LAYERS

        def raw_weight(w):
            l = w // 2
            return (W1[l].rearrange("(k p) f -> p k f", p=P) if w % 2 == 0
                    else W2[l].rearrange("(m p) d -> p m d", p=P))

        def stage_view(w):
            return stage[w % 2].rearrange("p (a b) -> p a b", a=KD if w % 2 == 0 else M)

        def slots_of(engine, slot):
            for s in range(-2, FIRST):
                slot(Slot(0, s, rounds))
            with engine.Fori(0, rounds - 1) as r:
                for s in range(FIRST, FIRST + ROUND):
                    slot(Slot(r, s, rounds))
            for s in range(FIRST, FIRST + ROUND):
                slot(Slot(rounds - 1, s, rounds))

        block = ctx.enter_context(nc.Block())

        @block.sync
        def _(sp_eng):
            def load_x(r, b):
                g = r * BUFS + b
                sp_eng.dma_start(xb[:, b], x_g[g]).then_inc(x_in[b], 16)

            def load_weight(w):
                if w >= 2:
                    sp_eng.wait_ge(S["split_lo"], w - 1)
                sp_eng.dma_start(stage_view(w), raw_weight(w)).then_inc(w_in[w % 2], 16)

            sp_eng.dma_start(col_rows[0:LAYERS * M], b1.rearrange("l (m p) -> (l m) p", p=P)).then_inc(
                S["col_rows_in"], 16)
            o = LAYERS * M
            for v in (g1, beta1):
                sp_eng.dma_start(col_rows[o:o + LAYERS * KD], v.rearrange("l (k p) -> (l k) p", p=P)).then_inc(
                    S["col_rows_in"], 16)
                o += LAYERS * KD
            load_x(0, 0)
            sp_eng.dma_start(adj_a[:], adj_g[0]).then_inc(S["adj_a_in"], 16)

            def row(v, n):
                return v.rearrange("(o l) d -> o (l d)", o=1).broadcast_to([P, n])

            def flat(t):
                return t[:, :, :].rearrange("p l d -> p (l d)")

            sp_eng.dma_start(flat(score_w), row(attn_w, LAYERS * 2 * D)).then_inc(S["rows_in"], 16)
            sp_eng.dma_start(score_b[:], attn_b.rearrange("(o l) -> o l", o=1).broadcast_to([P, LAYERS])).then_inc(
                S["rows_in"], 16)
            load_weight(0)
            load_weight(1)
            load_x(0, 1)
            sp_eng.dma_start(flat(g1_row), row(g1, LAYERS * D)).then_inc(S["beta_in"], 16)
            sp_eng.dma_start(flat(hb_row), row(beta1, LAYERS * D)).then_inc(S["beta_in"], 16)
            sp_eng.dma_start(flat(beta_tmp), row(b2, LAYERS * D)).then_inc(S["beta_in"], 16)
            sp_eng.dma_start(flat(g2_row), row(g2, LAYERS * D)).then_inc(S["beta_in"], 16)
            sp_eng.dma_start(flat(be2_row), row(beta2, LAYERS * D)).then_inc(S["beta_in"], 16)
            load_x(0, 2)
            load_x(0, 3)
            sp_eng.dma_start(adj_t[:], adj_g[0]).then_inc(S["adj_t_in"], 16)
            sp_eng.dma_start(gat_w[:], gat_a.rearrange("(o d) c -> o (d c)", o=1).broadcast_to([P, 2 * D])).then_inc(
                S["gw_in"], 16)
            sp_eng.dma_start(gw[:], gat_W.rearrange("(k p) d -> p k d", p=P)).then_inc(S["gw_in"], 16)
            for o_sem in out_in:
                sp_eng.sem_inc(o_sem, 16)

            def slot(j):
                r = j.r
                if j.starting:
                    for w in (2 * j.s + 6, 2 * j.s + 7):
                        if w < N_SPLITS and j.s > -2:
                            load_weight(w - 2)
                if isinstance(r, int) and r == 0 and j.s == 1:
                    load_weight(4)
                    load_weight(5)
                    sp_eng.wait_ge(S["hb_ready"], 1)
                    sp_eng.dma_start(xr[:], x_g[0]).then_inc(S["xr_in"], 16)
                if j.fresh:
                    sp_eng.wait_ge(S["mask_edges"], upto_gat(r, j.fresh - 1))
                    sp_eng.dma_start(adj_a[:], adj_g[group_of(r, j.fresh)]).then_inc(S["adj_a_in"], 16)
                if j.gat_sum is not None:
                    n = group_of(r, j.gat_sum)
                    sp_eng.wait_ge(S["u_added"], upto_gat(r, j.gat_sum))
                    if not (isinstance(r, int) and n + BUFS >= groups):
                        load_x(r + 1, buf_of(j.gat_sum))
                    if not (isinstance(r, int) and n + 1 >= groups):
                        sp_eng.dma_start(xr[:], x_g[n + 1]).then_inc(S["xr_in"], 16)
                if j.gat_a is not None and not (isinstance(r, int) and group_of(r, j.gat_a) + 1 >= groups):
                    sp_eng.wait_ge(S["m01_ready"], upto_gat(r, j.gat_a, 2))
                    sp_eng.dma_start(adj_t[:], adj_g[group_of(r, j.gat_a) + 1]).then_inc(S["adj_t_in"], 16)
                if j.gat_b is not None:
                    n = group_of(r, j.gat_b)
                    b = u_of(j.gat_b)
                    sp_eng.wait_ge(normed["out"], upto_gat(r, j.gat_b))
                    sp_eng.dma_start(out_g[n], u[:, b]).then_inc(out_in[b], 16)

            slots_of(sp_eng, slot)
            for i, o_sem in enumerate(out_in):
                sp_eng.wait_ge(o_sem, 16 * (-(-(BUFS - i) // U_BUFS) * rounds + 1))

        @block.gpsimd
        def _(pool):
            pool.memset(ident[:], 0.0).then_inc(S["ident_ready"], 1)
            pool.memset(half[:], -0.5).then_inc(S["consts_ready"], 1)
            pool.memset(mask[:, :, :, :], OFF).then_inc(S["mask_ready0"], 1)
            pool.wait_ge(S["ident_ready"], 1)
            pool.affine_select(out=ident[:], in_=ident[:], compare_op=ALU.not_equal, fill=1.0, base=0,
                               pattern=[[-1, P]], channel_multiplier=1).then_inc(S["ident_ready"], 1)
            pool.memset(m01[:, :, :], 0.0).then_inc(S["mask_ready0"], 1)
            pool.memset(gat_off[:], OFF).then_inc(S["consts_ready"], 1)
            pool.wait_ge(S["consts_ready"], 2)
            pool.wait_ge(S["beta_in"], 16 * 5)
            pool.tensor_tensor(hb_row[:], hb_row[:], beta_tmp, ALU.add).then_inc(S["hb_ready"], 1)
            pool.wait_ge(S["hb_ready"], 1)

            def power(name, count):
                pool.wait_ge(var_ready[name], count)
                pool.tensor_tensor(rd[name][:], ve[name][:], half[:], ALU.pow).then_inc(dev_ready[name], 1)

            def gains(s, r, gain, bias, scaled, ready):
                b, l = buf_of(s), layer_of(s)
                pool.tensor_tensor(xb[:, b], xb[:, b], gain[:, l:l + 1, :].broadcast_to([P, T, D]),
                                   ALU.mult).then_inc(scaled, 1)
                pool.wait_ge(scaled, upto(r, s))
                pool.tensor_tensor(xb[:, b], xb[:, b], bias[:, l:l + 1, :].broadcast_to([P, T, D]),
                                   ALU.add).then_inc(ready, 1)

            def slot(j):
                r = j.r
                if j.norm is not None:
                    power("mlp", upto(r, j.norm))
                    pool.wait_ge(normed["mlp"], upto(r, j.norm))
                    gains(j.norm, r, g2_row, be2_row, S["x_scaled"], S["x_ready"])
                if j.mix is not None:
                    power("mix", upto(r, j.mix))
                if j.gat_sum is not None:
                    b = buf_of(j.gat_sum)
                    pool.wait_ge(S["x_ready"], upto(r, j.gat_sum))
                    pool.wait_ge(S["xr_in"], upto_gat(r, j.gat_sum, 16))
                    stores = -(-(BUFS - u_of(b)) // U_BUFS)
                    pool.wait_ge(out_in[u_of(b)], r * (16 * stores) + 16 * (b // U_BUFS + 1))
                    pool.tensor_tensor(u[:, u_of(b)], xb[:, b], xr[:], ALU.add).then_inc(S["u_added"], 1)
                if j.gat_a is not None:
                    power("u", upto_gat(r, j.gat_a))
                if j.mix is not None:
                    pool.wait_ge(S["z_turned"], upto(r, j.mix, KD))
                    gains(j.mix, r, g1_row, hb_row, S["h_scaled"], S["h_ready"])
                if j.gat_b is not None:
                    b = u_of(j.gat_b)
                    pool.wait_ge(S["gmix_leaky"], upto_gat(r, j.gat_b, 2))
                    pool.tensor_tensor(u[:, b], u[:, b], wh, ALU.add).then_inc(S["out_added"], 1)
                    power("out", upto_gat(r, j.gat_b))

            slots_of(pool, slot)

        @block.scalar
        def _(act):
            def gelu(r, s, m):
                l = layer_of(s)
                c = l * M + m
                act.wait_ge(S["hid_done"], upto(r, s, M, m + 1))
                if m >= 4:
                    act.wait_ge(S["mlp2_done"], upto(r, s, M, m - 3))
                elif not (isinstance(r, int) and r == 0 and s == 0):
                    act.wait_ge(S["mlp2_done"], upto(r, s, M, m - 3))
                act.activation(gh[:, m % 4], hid[:, m % 2], ACT.Gelu, bias=cols[:, c:c + 1])
                if m >= 2 or not (isinstance(r, int) and r == 0 and s == 0):
                    act.wait_ge(S["gl_ready"], upto(r, s, M, m - 1))
                act.activation(gt[:, m % 2], hid[:, m % 2], ACT.Gelu, bias=cols[:, c:c + 1]).then_inc(
                    S["gelu_done"], 1)

            def slot(j):
                r = j.r

                def gelus(*ms):
                    if j.mlp is not None:
                        for m in ms:
                            gelu(r, j.mlp, m)

                gelus(0, 1)
                if j.score is not None:
                    act.wait_ge(S["spread_done"], upto(r, j.score))
                    for t in range(T):
                        a = act.activation(sp[:, t], spread[:, t], ACT.Identity, bias=sc[:, t:t + 1])
                    a.then_inc(S["scores_sum"], 1)
                gelus(2)
                if j.gat_b is not None:
                    act.wait_ge(S["gspread_done"], upto_gat(r, j.gat_b))
                    for t in range(T):
                        a = act.activation(gsp[:, t], spread[:, t], ACT.Identity, bias=gsc[:, T + t:T + t + 1])
                    a.then_inc(S["gscores_sum"], 1)
                gelus(3)
                if j.score is not None:
                    act.wait_ge(S["negmax"], upto(r, j.score))
                    for t in range(T):
                        a = act.activation(sp[:, t], sp[:, t], ACT.Exp, bias=nm[:, t:t + 1],
                                           accum_out=rs[:, t:t + 1])
                    a.then_inc(S["exp_done"], 1)
                if j.gat_b is not None:
                    act.wait_ge(S["gnegmax"], upto_gat(r, j.gat_b))
                    for t in range(T):
                        a = act.activation(gsp[:, t], gsp[:, t], ACT.Exp, bias=gnm[:, t:t + 1],
                                           accum_out=grs[:, t:t + 1])
                    a.then_inc(S["gexp_done"], 1)
                gelus(4, 5)
                if j.gat_b is not None:
                    for h in range(2):
                        act.wait_ge(S["gmix_done"], upto_gat(r, j.gat_b, 2, h + 1))
                        act.activation(wh[:, 2 * h:2 * h + 2], big_t[:, 2 * h:2 * h + 2], ACT.Copy,
                                       scale=SLOPE).then_inc(S["gmix_scaled"], 1)
                if j.score is not None:
                    act.wait_ge(S["probs_turned"], upto(r, j.score))
                    act.activation(pt[:, :, :], turn[:, :, :], ACT.Copy).then_inc(S["probs_ready"], 1)
                if j.mix is not None:
                    l = layer_of(j.mix)
                    for k in range(KD):
                        c = LAYERS * M + l * KD + k
                        cb = c + LAYERS * KD
                        act.wait_ge(S["z_turned"], upto(r, j.mix, KD, k + 1))
                        act.activation(hth[:, j.mix % 2, k], big_k[:, k], ACT.Identity, bias=cols[:, cb:cb + 1],
                                       scale=cols[:, c:c + 1])
                        act.activation(ht32[:, k], big_k[:, k], ACT.Identity, bias=cols[:, cb:cb + 1],
                                       scale=cols[:, c:c + 1]).then_inc(S["ht_ready"], 1)
                gelus(6)
                if j.gat_a is not None:
                    for k in range(KD):
                        act.wait_ge(S["ut_turned"], upto_gat(r, j.gat_a, KD, k + 1))
                        act.activation(ut[:, k], big_k[:, k], ACT.Copy).then_inc(S["ut_ready"], 1)
                gelus(7)
                if j.gat_a is not None:
                    if j.gat_b is not None:
                        act.wait_ge(S["out_added"], upto_gat(r, j.gat_b))
                    for h in range(2):
                        act.wait_ge(S["wh_done"], upto_gat(r, j.gat_a, 2, h + 1))
                        act.activation(wh[:, 2 * h:2 * h + 2], big_t[:, 2 * h:2 * h + 2], ACT.Copy).then_inc(
                            S["wh_ready"], 1)

            act.wait_ge(S["cols_ready"], 1)
            slots_of(act, slot)

        @block.tensor
        def _(pe):
            pe.wait_ge(S["ident_ready"], 2)
            pe.wait_ge(S["col_rows_in"], 16 * 3)
            pe.transpose(turn[:, 0, 0:NCOL], col_rows[:], ident[0:NCOL, 0:NCOL]).then_inc(S["cols_turned"], 1)
            pe.wait_ge(S["cols_ready"], 2)

            def mlp1(r, s, m):
                l, b = layer_of(s), s % 2
                if m == 0:
                    pe.wait_ge(S["htl_ready"], upto(r, s, KD))
                if m >= 2 or not (isinstance(r, int) and r == 0 and s == 0):
                    pe.wait_ge(S["gelu_done"], upto(r, s, M, m - 1))
                f = slice(m * P, (m + 1) * P)
                for k in range(KD):
                    pe.matmul(hid[:, m % 2], w1h[:, l, k, f], hth[:, b, k], start=(k == 0), stop=False)
                    pe.matmul(hid[:, m % 2], w1h[:, l, k, f], htl[:, b, k], start=False, stop=False)
                    a = pe.matmul(hid[:, m % 2], w1l[:, l, k, f], hth[:, b, k], start=False, stop=(k == KD - 1))
                a.then_inc(S["hid_done"], 1)

            def mlp2_part(s, m, tiles):
                l = layer_of(s)
                for t in tiles:
                    n = slice(t * P, (t + 1) * P)
                    pe.matmul(ff[:, t], gh[:, m % 4, n], w2h[:, l, m], start=(m == 0 and t % 2 == 0), stop=False,
                              skip_group_check=True)
                    pe.matmul(ff[:, t], gh[:, m % 4, n], w2l[:, l, m], start=False, stop=False,
                              skip_group_check=True)
                    a = pe.matmul(ff[:, t], gl[:, m % 4, n], w2h[:, l, m], start=False, stop=(m == M - 1),
                                  skip_group_check=True)
                return a

            def mlp2(r, s, m):
                pe.wait_ge(S["gl_ready"], upto(r, s, M, m + 1))
                if m == 0 and not (isinstance(r, int) and r == 0 and s == 0):
                    pe.wait_ge(S["ff_added"], upto(r, s - 1, 2))
                mlp2_part(s, m, range(T)).then_inc(S["mlp2_done"], 1)

            def mlp2_last(r, s, first):
                pe.wait_ge(S["gl_ready"], upto(r, s, M))
                for h in range(2):
                    for m in range(first, M):
                        a = mlp2_part(s, m, (2 * h, 2 * h + 1))
                        if h == 1 and m < M - 1:
                            a.then_inc(S["mlp2_done"], 1)
                    a.then_inc(S["ff_done"], 1)
                pe.nop().then_inc(S["mlp2_done"], 1)

            def slot(j):
                r = j.r

                def first_half(*ms):
                    if j.mlp is not None:
                        for m in ms:
                            mlp1(r, j.mlp, m)

                def second_half(m):
                    if j.mlp is not None:
                        mlp2(r, j.mlp, m)

                first_half(0, 1)
                if j.mix is not None:
                    b = buf_of(j.mix)
                    pe.wait_ge(S["probs_ready"], upto(r, j.mix))
                    before = Slot(r, j.s - 1, rounds)
                    if before.gat_a is not None:
                        pe.wait_ge(S["wh_ready"], upto_gat(r, before.gat_a, 2))
                    elif before.mix is not None:
                        pe.wait_ge(S["ht_ready"], upto(r, before.mix, KD))
                    for t in range(T):
                        a = pe.matmul(big_t[:, t], pt[:, t], xb[:, b, t], start=True, stop=True)
                        if t % 2:
                            a.then_inc(S["mix_done"], 1)
                first_half(2)
                second_half(0)
                if j.score is not None:
                    pe.wait_ge(S["scores_in"], upto(r, j.score))
                    for t in range(T):
                        a = pe.transpose(spread[:, t], sc[:, T + t:T + t + 1].broadcast_to([P, P]), ident[:])
                    a.then_inc(S["spread_done"], 1)
                first_half(3)
                if j.gat_b is not None:
                    pe.wait_ge(S["gscores_in"], upto_gat(r, j.gat_b))
                    if j.score is not None:
                        pe.wait_ge(S["scores_sum"], upto(r, j.score))
                    for t in range(T):
                        a = pe.transpose(spread[:, t], gsc[:, t:t + 1].broadcast_to([P, P]), ident[:])
                    a.then_inc(S["gspread_done"], 1)
                second_half(1)
                if j.gat_a is not None:
                    pe.wait_ge(S["m01_ready"], upto_gat(r, j.gat_a, 2))
                    for t in range(T):
                        a = pe.transpose(turn_b[:, t], m01[:, t], ident_b[:])
                    a.then_inc(S["masks_turned"], 1)
                first_half(4)
                second_half(2)
                if j.gat_b is not None:
                    b = u_of(j.gat_b)
                    pe.wait_ge(S["gprobs"], upto_gat(r, j.gat_b))
                    if j.mix is not None:
                        pe.wait_ge(S["mix_added"], upto(r, j.mix, T))
                    for t in range(T):
                        a = pe.matmul(big_t[:, t], gsp[:, t], wh[:, t], start=True, stop=True)
                        if t % 2:
                            a.then_inc(S["gmix_done"], 1)
                first_half(5)
                if j.score is not None:
                    pe.wait_ge(S["exp_done"], upto(r, j.score))
                    if j.gat_a is not None:
                        pe.wait_ge(S["ga_ready"], upto_gat(r, j.gat_a))
                    for t in range(T):
                        a = pe.transpose(turn[:, t], sp[:, t], ident[:])
                    a.then_inc(S["probs_turned"], 1)
                second_half(3)
                if j.mix is not None:
                    b = buf_of(j.mix)
                    pe.wait_ge(normed["mix"], upto(r, j.mix))
                    if j.gat_b is not None:
                        pe.wait_ge(S["gmix_leaky"], upto_gat(r, j.gat_b, 2))
                    for k in range(KD):
                        for t in range(T):
                            a = pe.transpose(big_k[:, k, t * P:(t + 1) * P], xb[:, b, t, k * P:(k + 1) * P], ident[:])
                        a.then_inc(S["z_turned"], 1)
                first_half(6)
                second_half(4)
                if j.gat_a is not None:
                    b = u_of(j.gat_a)
                    pe.wait_ge(normed["u"], upto_gat(r, j.gat_a))
                    if j.mix is not None:
                        pe.wait_ge(S["ht_ready"], upto(r, j.mix, KD))
                    elif j.gat_b is not None:
                        pe.wait_ge(S["gmix_leaky"], upto_gat(r, j.gat_b, 2))
                    for k in range(KD):
                        for t in range(T):
                            a = pe.transpose(big_k[:, k, t * P:(t + 1) * P], u[:, b, t, k * P:(k + 1) * P], ident[:])
                        a.then_inc(S["ut_turned"], 1)
                first_half(7)
                if j.gat_a is not None:
                    pe.wait_ge(S["ut_ready"], upto_gat(r, j.gat_a, KD))
                    for t in range(T):
                        for k in range(KD):
                            a = pe.matmul(big_t[:, t], ut[:, k, t * P:(t + 1) * P], gw[:, k], start=(k == 0),
                                          stop=(k == KD - 1))
                        if t % 2:
                            a.then_inc(S["wh_done"], 1)
                if j.mlp is not None:
                    mlp2_last(r, j.mlp, 5)

            pe.wait_ge(S["gw_in"], 32)
            slots_of(pe, slot)

        @block.vector
        def _(dve):
            dve.wait_ge(S["cols_turned"], 1)
            dve.tensor_copy(cols[:], turn[:, 0, 0:NCOL]).then_inc(S["cols_ready"], 1)
            dve.wait_ge(S["ident_ready"], 2)
            dve.tensor_copy(ident_b[:], ident[:]).then_inc(S["cols_ready"], 1)
            for a in range(per_tile):
                i = slice(a * nodes, (a + 1) * nodes)
                dve.tensor_copy(eye[i, :], ident[i, i]).then_inc(S["cols_ready"], 1)
            dve.wait_ge(S["cols_ready"], 2 + per_tile)
            dve.wait_ge(S["mask_ready0"], 2)
            dve.wait_ge(S["consts_ready"], 2)
            for a in range(per_tile):
                i = slice(a * nodes, (a + 1) * nodes)
                dve.memset(gat_off[i, i], GAT_OFF).then_inc(S["consts_ready"], 1)
            dve.wait_ge(S["rows_in"], 32)

            def wait_alone(s, count):
                dve.wait_ge(S["cols_ready"], 2)
                dve.wait_ge(s, count)

            def split_weight(w):
                l = w // 2
                hi, lo = ((w1h, w1l) if w % 2 == 0 else (w2h, w2l))
                dve.wait_ge(w_in[w % 2], 16 * (w // 2 + 1))
                dve.tensor_copy(hi[:, l], stage_view(w)).then_inc(S["split_hi"], 1)
                dve.wait_ge(S["split_hi"], w + 1)
                dve.tensor_tensor(lo[:, l], stage_view(w), hi[:, l].bitcast(F32), ALU.subtract).then_inc(
                    S["split_lo"], 1)

            def statistics(name, y, count, wait_tile):
                for t in range(T):
                    wait_tile(t)
                    a = dve.bn_stats(st[name][:, t], y[:, t])
                a.then_inc(stats_done[name], 1)
                wait_alone(stats_done[name], count)
                for t in range(T):
                    a = dve.bn_aggr(mv[name][:, t], st[name][:, t])
                a.then_inc(mean_done[name], 1)
                dve.wait_ge(mean_done[name], count)
                dve.tensor_scalar(ve[name][:], mv[name][:, :, 1], EPS, None, ALU.add).then_inc(var_ready[name], 1)

            def normalise(name, y, count):
                dve.wait_ge(dev_ready[name], count)
                for t in range(T):
                    a = dve.tensor_scalar(y[:, t], y[:, t], mv[name][:, t, 0:1], rd[name][:, t:t + 1],
                                          ALU.subtract, ALU.mult)
                a.then_inc(normed[name], 1)

            def pair_scores(src, w_row, dst, bias, done):
                for c in range(2):
                    for t in range(T):
                        a = dve.tensor_tensor_reduce(unread[:, c * T + t], src[:, t], w_row[:, c * D:(c + 1) * D], 1.0,
                                                     bias if c == 0 else 0.0, ALU.mult, ALU.add,
                                                     dst[:, c * T + t:c * T + t + 1])
                a.then_inc(done, 1)

            def slot(j):
                r = j.r

                def gl_part(*ms):
                    if j.mlp is not None:
                        for m in ms:
                            dve.wait_ge(S["gelu_done"], upto(r, j.mlp, M, m + 1))
                            if m >= 4 or not (isinstance(r, int) and r == 0 and j.mlp == 0):
                                dve.wait_ge(S["mlp2_done"], upto(r, j.mlp, M, m - 3))
                            dve.tensor_tensor(gl[:, m % 4], gt[:, m % 2], gh[:, m % 4].bitcast(F32),
                                              ALU.subtract).then_inc(S["gl_ready"], 1)

                if isinstance(r, int) and r == 0 and j.s in (-1, 0, 1):
                    split_weight(2 * (j.s + 1))
                    split_weight(2 * (j.s + 1) + 1)
                if j.norm is not None:
                    b = buf_of(j.norm)
                    dve.wait_ge(S["h_ready"], upto(r, j.norm))
                    for h in range(2):
                        y = xb[:, b, 2 * h:2 * h + 2]
                        dve.wait_ge(S["ff_done"], upto(r, j.norm, 2, h + 1))
                        dve.tensor_tensor(y, ff[:, 2 * h:2 * h + 2], y, ALU.add).then_inc(S["ff_added"], 1)
                    statistics("mlp", xb[:, b], upto(r, j.norm),
                               lambda t: dve.wait_ge(S["ff_added"], upto(r, j.norm, 2, t // 2 + 1)))
                if j.score is not None:
                    b, l = buf_of(j.score), layer_of(j.score)
                    if l == 0:
                        dve.wait_ge(x_in[b], r * 16 + 16 * (j.score // ROUND + 1))
                    else:
                        dve.wait_ge(S["x_ready"], upto(r, j.score - BUFS))
                    pair_scores(xb[:, b], score_w[:, l], sc, score_b[:, l:l + 1], S["scores_in"])
                if j.norm is not None:
                    normalise("mlp", xb[:, buf_of(j.norm)], upto(r, j.norm))
                gl_part(0)
                if j.gat_b is not None:
                    dve.wait_ge(S["wh_ready"], upto_gat(r, j.gat_b, 2))
                    if j.score is not None:
                        dve.wait_ge(S["scores_in"], upto(r, j.score))
                    pair_scores(wh, gat_w[:], gsc, 0.0, S["gscores_in"])
                if j.fresh is not None:
                    b = buf_of(j.fresh)
                    dve.wait_ge(S["adj_a_in"], upto_gat(r, j.fresh, 16))
                    dve.tensor_tensor(adj_e[:], adj_a[:], eye[:].rearrange("p (o j) -> p o j", o=1).broadcast_to(
                        [P, T, nodes]), ALU.add).then_inc(S["mask_edges"], 1)
                    dve.wait_ge(S["mask_edges"], upto_gat(r, j.fresh))
                    for a in range(per_tile):
                        i = slice(a * nodes, (a + 1) * nodes)
                        dve.tensor_scalar(mask[i, b, :, i], adj_e[i], 0.0, OFF, ALU.is_le, ALU.mult).then_inc(
                            S["mask_ready"], 1)
                if j.mix is not None:
                    b = buf_of(j.mix)
                    dve.wait_ge(S["sum_inverse"], upto(r, j.mix))
                    for t in range(T):
                        if t % 2 == 0:
                            dve.wait_ge(S["mix_done"], upto(r, j.mix, 2, t // 2 + 1))
                        dve.scalar_tensor_tensor(out=xb[:, b, t], in0=big_t[:, t], scalar=ri[:, t:t + 1],
                                                 in1=xb[:, b, t], op0=ALU.mult, op1=ALU.add).then_inc(
                                                     S["mix_added"], 1)
                    statistics("mix", xb[:, b], upto(r, j.mix),
                               lambda t: dve.wait_ge(S["mix_added"], upto(r, j.mix, T, t + 1)))
                gl_part(1)
                if j.score is not None:
                    b = buf_of(j.score)
                    if j.fresh is not None:
                        dve.wait_ge(S["mask_ready"], upto_gat(r, j.fresh, per_tile))
                    dve.wait_ge(S["scores_sum"], upto(r, j.score))
                    dve.scalar_tensor_tensor(out=sp[:, :, :], in0=sp[:, :, :], scalar=SLOPE, in1=sp[:, :, :],
                                             op0=ALU.mult, op1=ALU.max).then_inc(S["scores_leaky"], 1)
                    wait_alone(S["scores_leaky"], upto(r, j.score))
                    for t in range(T):
                        a = dve.tensor_tensor_reduce(sp[:, t], sp[:, t], mask[:, b, t], 1.0, OFF, ALU.add, ALU.max,
                                                     mx[:, t:t + 1])
                    a.then_inc(S["max_done"], 1)
                gl_part(2)
                if j.score is not None:
                    dve.wait_ge(S["max_done"], upto(r, j.score))
                    dve.tensor_scalar(nm[:], mx[:], -1.0, None, ALU.mult).then_inc(S["negmax"], 1)
                if j.mix is not None:
                    normalise("mix", xb[:, buf_of(j.mix)], upto(r, j.mix))
                if j.gat_b is not None:
                    dve.wait_ge(S["gscores_sum"], upto_gat(r, j.gat_b))
                    dve.scalar_tensor_tensor(out=gsp[:, :, :], in0=gsp[:, :, :], scalar=SLOPE, in1=gsp[:, :, :],
                                             op0=ALU.mult, op1=ALU.max).then_inc(S["gleaky"], 1)
                    dve.wait_ge(S["gleaky"], upto_gat(r, j.gat_b))
                    dve.tensor_tensor(gsp[:, :, :], gsp[:, :, :], gm[:, :, :], ALU.mult).then_inc(S["gmasked"], 1)
                    wait_alone(S["gmasked"], upto_gat(r, j.gat_b))
                    for t in range(T):
                        a = dve.tensor_tensor_reduce(gsp[:, t], gsp[:, t], ga[:, t], 1.0, OFF, ALU.add, ALU.max,
                                                     gmx[:, t:t + 1])
                    a.then_inc(S["gmax_done"], 1)
                    dve.wait_ge(S["gmax_done"], upto_gat(r, j.gat_b))
                    dve.tensor_scalar(gnm[:], gmx[:], -1.0, None, ALU.mult).then_inc(S["gnegmax"], 1)
                if j.gat_a is not None:
                    dve.wait_ge(S["adj_t_in"], upto_gat(r, j.gat_a, 16))
                    for a in range(per_tile):
                        i = slice(a * nodes, (a + 1) * nodes)
                        dve.tensor_scalar(m01[i, :, i], adj_t[i], 0.0, None, ALU.is_gt).then_inc(S["m01_ready"], 1)
                gl_part(3)
                if j.gat_a is not None:
                    dve.wait_ge(S["masks_turned"], upto_gat(r, j.gat_a))
                    dve.tensor_copy(gm[:, :, :], turn_b).then_inc(S["gm_ready"], 1)
                    dve.scalar_tensor_tensor(
                        out=ga[:, :, :], in0=turn_b, scalar=-GAT_OFF,
                        in1=gat_off[:].rearrange("p (o n) -> p o n", o=1).broadcast_to([P, T, P]),
                        op0=ALU.mult, op1=ALU.add).then_inc(S["ga_ready"], 1)
                if j.gat_b is not None:
                    dve.wait_ge(S["gexp_done"], upto_gat(r, j.gat_b))
                    dve.reciprocal(gri[:], grs[:]).then_inc(S["gsum_inverse"], 1)
                    dve.wait_ge(S["gsum_inverse"], upto_gat(r, j.gat_b))
                    for t in range(T):
                        a = dve.tensor_scalar(gsp[:, t], gsp[:, t], gri[:, t:t + 1], None, ALU.mult)
                    a.then_inc(S["gprobs"], 1)
                if j.gat_a is not None:
                    b = u_of(j.gat_a)
                    dve.wait_ge(S["u_added"], upto_gat(r, j.gat_a))
                    statistics("u", u[:, b], upto_gat(r, j.gat_a), lambda t: None)
                gl_part(4)
                if j.gat_a is not None:
                    normalise("u", u[:, u_of(j.gat_a)], upto_gat(r, j.gat_a))
                gl_part(5)
                if j.gat_b is not None:
                    for h in range(2):
                        dve.wait_ge(S["gmix_scaled"], upto_gat(r, j.gat_b, 2, h + 1))
                        w = wh[:, 2 * h:2 * h + 2]
                        dve.tensor_tensor(w, big_t[:, 2 * h:2 * h + 2], w, ALU.max).then_inc(S["gmix_leaky"], 1)
                if j.score is not None:
                    dve.wait_ge(S["exp_done"], upto(r, j.score))
                    dve.reciprocal(ri[:], rs[:]).then_inc(S["sum_inverse"], 1)
                if j.mix is not None:
                    for k in range(KD):
                        dve.wait_ge(S["ht_ready"], upto(r, j.mix, KD, k + 1))
                        dve.tensor_tensor(htl[:, j.mix % 2, k], ht32[:, k], hth[:, j.mix % 2, k].bitcast(F32),
                                          ALU.subtract).then_inc(S["htl_ready"], 1)
                gl_part(6)
                if j.gat_b is not None:
                    b = u_of(j.gat_b)
                    dve.wait_ge(S["out_added"], upto_gat(r, j.gat_b))
                    statistics("out", u[:, b], upto_gat(r, j.gat_b), lambda t: None)
                gl_part(7)
                if j.gat_b is not None:
                    normalise("out", u[:, u_of(j.gat_b)], upto_gat(r, j.gat_b))

            slots_of(dve, slot)


_INS = ['x', 'adj', 'L0_gnn_attn_w', 'L0_gnn_attn_b', 'L0_gnn_W1', 'L0_gnn_b1', 'L0_gnn_W2', 'L0_gnn_b2',
        'L0_gnn_g1', 'L0_gnn_beta1', 'L0_gnn_g2', 'L0_gnn_beta2', 'L1_gnn_W', 'L1_gnn_a']


def kernel(**inputs):
    import numpy as _np
    import concourse.bacc as _bacc
    from concourse import mybir as _mybir
    from concourse.bass_utils import run_bass_kernel_spmd as _run

    nc = _bacc.Bacc("TRN2", target_bir_lowering=False, num_devices=1, dynamic_dma_scratch_size=1024)
    arrays, args = {}, []
    for name in _INS:
        a = _np.ascontiguousarray(inputs[name])
        arrays[f"in_{name}_dram"] = a
        args.append(nc.dram_tensor(f"in_{name}_dram", a.shape, _mybir.dt.from_np(a.dtype), kind="ExternalInput").ap())
    shape = tuple(inputs['x'].shape)
    args.append(nc.dram_tensor("out_0_dram", shape, _mybir.dt.float32, kind="ExternalOutput").ap())
    graph_net_kernel(nc, *args)
    r = _run(nc, [arrays], core_ids=[0])
    return r.results[0]["out_0_dram"]
```

```python
from contextlib import ExitStack

import concourse.bass as bass
from concourse import mybir

F32 = mybir.dt.float32
F32R = mybir.dt.float32r
BF16 = mybir.dt.bfloat16
I32 = mybir.dt.int32
ALU = mybir.AluOpType
ACT = mybir.ActivationFunctionType
AX = mybir.AxisListType

P = 128
T = 4
BUFS = 4
LAYERS = 3
ROUND = BUFS * LAYERS
FIRST = 5
EPS = 1e-5
SLOPE = 0.2
OFF = -3.0e38
GAT_OFF = -9.0e15


def layer_of(s):
    return (s % ROUND) // BUFS


def buf_of(s):
    return s % BUFS


def group_of(r, s):
    return r * BUFS + (BUFS * (s // ROUND) + s % BUFS)


def upto(r, s, per=1, part=None):
    return r * (ROUND * per) + (s * per + (per if part is None else part))


def upto_gat(r, s, per=1, part=None):
    return r * (BUFS * per) + ((BUFS * (s // ROUND) + s % BUFS) * per + (per if part is None else part))


class Slot:

    def __init__(self, r, s, rounds):
        q = (r if isinstance(r, int) else 1) * ROUND + s
        jobs = rounds * ROUND
        self.r, self.s = r, s
        self.mlp = s if 0 <= q < jobs else None
        self.norm = s - 1 if 0 <= q - 1 < jobs else None
        self.pair = s + 3 if 0 <= q + 3 < jobs else None
        self.score = s + 2 if 0 <= q + 2 < jobs else None
        self.mix = s + 1 if 0 <= q + 1 < jobs else None

        def last_layer(d):
            return s - d if 0 <= q - d < jobs and layer_of(s - d) == LAYERS - 1 else None

        self.gat_in = last_layer(0)
        self.gat_sum = last_layer(1)
        self.gat_stats = last_layer(2)
        self.gat_wh = last_layer(3)
        self.gat_soft = last_layer(4)
        self.gat_out = last_layer(5)
        self.fresh = self.pair if self.pair is not None and layer_of(self.pair) == 0 else None
        self.starting = s < 1 and isinstance(r, int) and r == 0


def graph_net_kernel(nc, x, adj, attn_w, attn_b, W1, b1, W2, b2, g1, beta1, g2, beta2, gat_W, gat_a, out):
    graphs, nodes, D = x.shape
    F = W1.shape[2]
    KD = D // P
    M = F // P
    per_tile = P // nodes
    groups = graphs // (per_tile * T)
    rounds = groups // BUFS
    NT = T * P
    assert groups % BUFS == 0 and nodes * per_tile == P and D * 2 == NT

    x_g = x.rearrange("(G t g) i d -> G (g i) t d", t=T, g=per_tile)
    adj_g = adj.rearrange("(G t g) i j -> G (g i) t j", t=T, g=per_tile)
    out_g = out.rearrange("(G t g) i d -> G (g i) t d", t=T, g=per_tile)

    with ExitStack() as ctx:
        def sb(name, shape, dt=F32):
            return ctx.enter_context(nc.sbuf_tensor(name, shape, dt))

        def ps(name, shape, dt=F32):
            return ctx.enter_context(nc.psum_tensor(name, shape, dt))

        def sem(name):
            return ctx.enter_context(nc.semaphore(name))

        w1h = sb("w1h", [P, LAYERS, KD, F], F32R)
        w1l = sb("w1l", [P, LAYERS, KD, F], F32R)
        w2h = sb("w2h", [P, LAYERS, M, D], F32R)
        w2l = sb("w2l", [P, LAYERS, M, D], F32R)
        gw = sb("gw", [P, KD, D])
        NCOL = LAYERS * (M + 2 * KD)
        cols = sb("cols", [P, NCOL])
        score_w = sb("score_w", [P, LAYERS, 2 * D])
        gat_w = sb("gat_w", [P, 2 * D])
        score_b = sb("score_b", [P, LAYERS])
        g1_row = sb("g1_row", [P, LAYERS, D])
        hb_row = sb("hb_row", [P, LAYERS, D])
        g2_row = sb("g2_row", [P, LAYERS, D])
        be2_row = sb("be2_row", [P, LAYERS, D])
        ident = sb("ident", [P, P])
        ident_b = sb("ident_b", [P, P], BF16)
        eye = sb("eye", [P, nodes])
        gat_off = sb("gat_off", [P, P])
        half = sb("half", [P, T])
        xb = sb("xb", [P, BUFS, T, D])
        ht32 = sb("ht32", [P, KD, NT])
        hth = sb("hth", [P, 2, KD, NT], F32R)
        htl = sb("htl", [P, 2, KD, NT], F32R)
        gt = sb("gt", [P, 2, NT])
        gh = sb("gh", [P, 4, NT], F32R)
        gl = sb("gl", [P, 4, NT], F32R)
        adj_a = sb("adj_a", [P, T, nodes], I32)
        adj_e = sb("adj_e", [P, T, nodes], BF16)
        mask = sb("mask", [P, BUFS, T, P], BF16)
        sc = sb("sc", [P, 2 * T])
        sp = sb("sp", [P, T, P])
        pt = sb("pt", [P, T, P])
        unread = sb("unread", [P, T, D], BF16)
        mx = sb("mx", [P, T])
        nm = sb("nm", [P, T])
        rs = sb("rs", [P, T])
        ri = sb("ri", [P, T])
        norm_names = ("mix", "mlp", "u", "out")
        st = {n: sb(f"st_{n}", [P, T, 6]) for n in norm_names}
        mv = {n: sb(f"mv_{n}", [P, T, 2]) for n in norm_names}
        ve = {n: sb(f"ve_{n}", [P, T]) for n in norm_names}
        rd = {n: sb(f"rd_{n}", [P, T]) for n in norm_names}
        nmean = {n: sb(f"nmean_{n}", [P, T]) for n in ("u", "out")}
        nb = {n: sb(f"nb_{n}", [P, T]) for n in ("u", "out")}
        u = sb("u", [P, BUFS, T, D])
        wh = sb("wh", [P, 2, T, D])
        ut = sb("ut", [P, KD, NT])
        adj_t = sb("adj_t", [P, T, nodes], I32)
        col_rows = adj_t[0:NCOL, :, :].rearrange("p t n -> p (t n)").bitcast(F32)[:, 0:P]
        m01 = sb("m01", [P, T, P], BF16)
        gm = m01
        ga = sb("ga", [P, T, P])
        gsc = sb("gsc", [P, 2 * T])
        gsp = sb("gsp", [P, T, P])
        gmx = sb("gmx", [P, T])
        gnm = sb("gnm", [P, T])
        grs = sb("grs", [P, T])
        gri = sb("gri", [P, T])
        stage = [u[:, 0:2, :, :].rearrange("p a t d -> p (a t d)"), wh[:, :, :, :].rearrange("p a t d -> p (a t d)")]
        beta_tmp = u[:, 2, 0:LAYERS, :]

        hid = ps("hid", [P, 2, NT])
        ff = ps("ff", [P, T, D])
        big = ps("big", [P, T * D])
        side = ps("side", [P, 2, T, P])
        spread = side[:, 0]
        turn = side[:, 1]
        wide = side[:, :, :, :].rearrange("p a t n -> p (a t n)").rearrange("p (t d) -> p t d", t=T)
        big_t = big[:, :].rearrange("p (t d) -> p t d", t=T)
        big_k = big[:, :].rearrange("p (k n) -> p k n", k=KD)
        turn_b = turn.rearrange("p t n -> p (t n)").bitcast(BF16)[:, 0:T * P].rearrange("p (t n) -> p t n", t=T)

        names = """col_rows_in rows_in beta_in gw_in
            adj_a_in adj_t_in ident_ready consts_ready mask_ready0 cols_turned cols_ready hb_ready
            split_hi split_lo mask_edges mask_ready
            scores_in spread_done scores_sum scores_leaky max_done negmax exp_done probs_turned
            probs_ready sum_inverse mix_done mix_added z_turned ht_ready htl_ready h_scaled h_ready
            hid_done gelu_done gl_ready mlp2_done ff_done ff_added x_scaled x_ready
            u_part u_added ut_turned ut_ready wh_done wh_ready m01_ready masks_turned gm_ready ga_ready
            gscores_in gspread_done gscores_sum gleaky gmasked gmax_done gnegmax gexp_done gsum_inverse
            gprobs gmix_done gmix_scaled gmix_leaky out_added""".split()
        S = {n: sem(n) for n in names}
        x_in = [sem(f"x_in{i}") for i in range(BUFS)]
        w_in = [sem(f"w_in{i}") for i in range(2)]
        u_in = [sem(f"u_in{i}") for i in range(BUFS)]
        out_in = [sem(f"out_stored{i}") for i in range(BUFS)]
        stats_done = {n: sem(f"stats_{n}") for n in norm_names}
        mean_done = {n: sem(f"mean_{n}") for n in norm_names}
        var_ready = {n: sem(f"var_{n}") for n in norm_names}
        dev_ready = {n: sem(f"dev_{n}") for n in norm_names}
        nb_ready = {n: sem(f"nb_{n}_ready") for n in ("u", "out")}
        normed = {n: sem(f"normed_{n}") for n in norm_names}

        N_SPLITS = 2 * LAYERS

        def raw_weight(w):
            l = w // 2
            return (W1[l].rearrange("(k p) f -> p k f", p=P) if w % 2 == 0
                    else W2[l].rearrange("(m p) d -> p m d", p=P))

        def stage_view(w):
            return stage[w % 2].rearrange("p (a b) -> p a b", a=KD if w % 2 == 0 else M)

        def slots_of(engine, slot):
            for s in range(-3, FIRST):
                slot(Slot(0, s, rounds))
            with engine.Fori(0, rounds - 1) as r:
                for s in range(FIRST, FIRST + ROUND):
                    slot(Slot(r, s, rounds))
            for s in range(FIRST, FIRST + ROUND):
                slot(Slot(rounds - 1, s, rounds))

        def wait_room(eng, r, s, m):
            if m >= 4:
                eng.wait_ge(S["mlp2_done"], upto(r, s, M - 1, m - 3))
            elif isinstance(r, int) and r == 0 and s == 0:
                return
            elif m < 3:
                eng.wait_ge(S["mlp2_done"], upto(r, s - 1, M - 1, m + 5))
            else:
                eng.wait_ge(S["ff_done"], upto(r, s - 1, 2))

        block = ctx.enter_context(nc.Block())

        @block.sync
        def _(sp_eng):
            def load_x(r, b):
                g = r * BUFS + b
                sp_eng.dma_start(xb[:, b], x_g[g]).then_inc(x_in[b], 16)

            def load_weight(w):
                if w >= 2:
                    sp_eng.wait_ge(S["split_lo"], w - 1)
                sp_eng.dma_start(stage_view(w), raw_weight(w)).then_inc(w_in[w % 2], 16)

            sp_eng.dma_start(col_rows[0:LAYERS * M], b1.rearrange("l (m p) -> (l m) p", p=P)).then_inc(
                S["col_rows_in"], 16)
            o = LAYERS * M
            for v in (g1, beta1):
                sp_eng.dma_start(col_rows[o:o + LAYERS * KD], v.rearrange("l (k p) -> (l k) p", p=P)).then_inc(
                    S["col_rows_in"], 16)
                o += LAYERS * KD
            load_x(0, 0)
            sp_eng.dma_start(adj_a[:], adj_g[0]).then_inc(S["adj_a_in"], 16)

            def row(v, n):
                return v.rearrange("(o l) d -> o (l d)", o=1).broadcast_to([P, n])

            def flat(t):
                return t[:, :, :].rearrange("p l d -> p (l d)")

            sp_eng.dma_start(flat(score_w), row(attn_w, LAYERS * 2 * D)).then_inc(S["rows_in"], 16)
            sp_eng.dma_start(score_b[:], attn_b.rearrange("(o l) -> o l", o=1).broadcast_to([P, LAYERS])).then_inc(
                S["rows_in"], 16)
            load_weight(0)
            load_weight(1)
            load_x(0, 1)
            sp_eng.dma_start(flat(g1_row), row(g1, LAYERS * D)).then_inc(S["beta_in"], 16)
            sp_eng.dma_start(flat(hb_row), row(beta1, LAYERS * D)).then_inc(S["beta_in"], 16)
            sp_eng.dma_start(flat(beta_tmp), row(b2, LAYERS * D)).then_inc(S["beta_in"], 16)
            sp_eng.dma_start(flat(g2_row), row(g2, LAYERS * D)).then_inc(S["beta_in"], 16)
            sp_eng.dma_start(flat(be2_row), row(beta2, LAYERS * D)).then_inc(S["beta_in"], 16)
            load_x(0, 2)
            load_x(0, 3)
            sp_eng.wait_ge(S["cols_turned"], 1)
            sp_eng.dma_start(adj_t[:], adj_g[0]).then_inc(S["adj_t_in"], 16)
            sp_eng.dma_start(gat_w[:], gat_a.rearrange("(o d) c -> o (d c)", o=1).broadcast_to([P, 2 * D])).then_inc(
                S["gw_in"], 16)
            sp_eng.dma_start(gw[:], gat_W.rearrange("(k p) d -> p k d", p=P)).then_inc(S["gw_in"], 16)
            for o_sem in out_in:
                sp_eng.sem_inc(o_sem, 16)

            def slot(j):
                r = j.r
                if j.starting:
                    for w in (2 * j.s + 6, 2 * j.s + 7):
                        if w < N_SPLITS and j.s > -2:
                            load_weight(w - 2)
                if isinstance(r, int) and r == 0 and j.s == 1:
                    load_weight(4)
                    load_weight(5)
                if isinstance(r, int) and r == 0 and j.s == FIRST - 1:
                    sp_eng.wait_ge(S["split_lo"], N_SPLITS)
                    sp_eng.wait_ge(S["hb_ready"], 1)
                if j.fresh:
                    sp_eng.wait_ge(S["mask_edges"], upto_gat(r, j.fresh - 1))
                    sp_eng.dma_start(adj_a[:], adj_g[group_of(r, j.fresh)]).then_inc(S["adj_a_in"], 16)
                if j.gat_in is not None:
                    b = buf_of(j.gat_in)
                    sp_eng.wait_ge(out_in[b], r * 16 + 16)
                    sp_eng.dma_start(u[:, b], x_g[group_of(r, j.gat_in)]).then_inc(u_in[b], 16)
                if j.gat_sum is not None and not (isinstance(r, int) and group_of(r, j.gat_sum) + BUFS >= groups):
                    sp_eng.wait_ge(S["u_added"], upto_gat(r, j.gat_sum))
                    load_x(r + 1, buf_of(j.gat_sum))
                if j.gat_out is not None:
                    b = buf_of(j.gat_out)
                    sp_eng.wait_ge(normed["out"], upto_gat(r, j.gat_out))
                    sp_eng.dma_start(out_g[group_of(r, j.gat_out)], u[:, b]).then_inc(out_in[b], 16)
                if j.gat_wh is not None and not (isinstance(r, int) and group_of(r, j.gat_wh) + 1 >= groups):
                    sp_eng.wait_ge(S["m01_ready"], upto_gat(r, j.gat_wh, per_tile))
                    sp_eng.dma_start(adj_t[:], adj_g[group_of(r, j.gat_wh) + 1]).then_inc(S["adj_t_in"], 16)

            slots_of(sp_eng, slot)
            for o_sem in out_in:
                sp_eng.wait_ge(o_sem, 16 * (rounds + 1))

        @block.gpsimd
        def _(pool):
            pool.memset(ident[:], 0.0).then_inc(S["ident_ready"], 1)
            pool.memset(half[:], -0.5).then_inc(S["consts_ready"], 1)
            pool.memset(mask[:, :, :, :], OFF).then_inc(S["mask_ready0"], 1)
            pool.wait_ge(S["ident_ready"], 1)
            pool.affine_select(out=ident[:], in_=ident[:], compare_op=ALU.not_equal, fill=1.0, base=0,
                               pattern=[[-1, P]], channel_multiplier=1).then_inc(S["ident_ready"], 1)
            pool.memset(m01[:, :, :], 0.0).then_inc(S["mask_ready0"], 1)
            pool.memset(gat_off[:], OFF).then_inc(S["consts_ready"], 1)
            pool.wait_ge(S["consts_ready"], 2)
            pool.wait_ge(S["beta_in"], 16 * 5)
            pool.tensor_tensor(hb_row[:], hb_row[:], beta_tmp, ALU.add).then_inc(S["hb_ready"], 1)
            pool.wait_ge(S["hb_ready"], 1)

            def power(name, count):
                pool.wait_ge(var_ready[name], count)
                pool.tensor_tensor(rd[name][:], ve[name][:], half[:], ALU.pow).then_inc(dev_ready[name], 1)

            def gain_mult(s, gain, scaled):
                b, l = buf_of(s), layer_of(s)
                pool.tensor_tensor(xb[:, b], xb[:, b], gain[:, l:l + 1, :].broadcast_to([P, T, D]),
                                   ALU.mult).then_inc(scaled, 1)

            def gain_add(r, s, bias, scaled, ready):
                b, l = buf_of(s), layer_of(s)
                pool.wait_ge(scaled, upto(r, s))
                pool.tensor_tensor(xb[:, b], xb[:, b], bias[:, l:l + 1, :].broadcast_to([P, T, D]),
                                   ALU.add).then_inc(ready, 1)

            def power_and_shift(name, count):
                power(name, count)
                pool.wait_ge(dev_ready[name], count)
                pool.tensor_tensor(nb[name][:], nmean[name][:], rd[name][:], ALU.mult).then_inc(nb_ready[name], 1)

            def slot(j):
                r = j.r
                if j.gat_out is not None:
                    pool.wait_ge(S["gsum_inverse"], upto_gat(r, j.gat_out))
                    pool.tensor_tensor(gsp[:, :, :], gsp[:, :, :], gri[:].rearrange("p (t o) -> p t o", o=1).broadcast_to(
                        [P, T, P]), ALU.mult).then_inc(S["gprobs"], 1)
                if j.norm is not None:
                    power("mlp", upto(r, j.norm))
                if j.gat_stats is not None:
                    power_and_shift("u", upto_gat(r, j.gat_stats))
                if j.norm is not None:
                    pool.wait_ge(normed["mlp"], upto(r, j.norm))
                    gain_mult(j.norm, g2_row, S["x_scaled"])
                    gain_add(r, j.norm, be2_row, S["x_scaled"], S["x_ready"])
                if j.mix is not None:
                    power("mix", upto(r, j.mix))
                if j.gat_out is not None:
                    b = buf_of(j.gat_out)
                    pool.wait_ge(S["gmix_leaky"], upto_gat(r, j.gat_out, 2))
                    pool.tensor_tensor(u[:, b], u[:, b], wh[:, b % 2], ALU.add).then_inc(S["out_added"], 1)
                if j.gat_sum is not None:
                    b = buf_of(j.gat_sum)
                    pool.wait_ge(S["x_ready"], upto(r, j.gat_sum))
                    pool.wait_ge(u_in[b], r * 16 + 16)
                    pool.tensor_tensor(u[:, b], u[:, b], xb[:, b], ALU.add).then_inc(S["u_added"], 1)
                if j.mix is not None:
                    for k in range(KD):
                        pool.wait_ge(S["ht_ready"], upto(r, j.mix, KD, k + 1))
                        pool.tensor_tensor(htl[:, j.mix % 2, k], ht32[:, k], hth[:, j.mix % 2, k].bitcast(F32),
                                           ALU.subtract).then_inc(S["htl_ready"], 1)
                if j.gat_soft is not None:
                    pool.wait_ge(S["gleaky"], upto_gat(r, j.gat_soft))
                    pool.wait_ge(S["gm_ready"], upto_gat(r, j.gat_soft))
                    pool.tensor_tensor(gsp[:, :, :], gsp[:, :, :], gm[:, :, :], ALU.mult).then_inc(S["gmasked"], 1)
                if j.gat_out is not None:
                    power_and_shift("out", upto_gat(r, j.gat_out))
                if j.mix is not None:
                    pool.wait_ge(S["z_turned"], upto(r, j.mix, KD))
                    gain_mult(j.mix, g1_row, S["h_scaled"])
                    gain_add(r, j.mix, hb_row, S["h_scaled"], S["h_ready"])

            slots_of(pool, slot)

        @block.scalar
        def _(act):
            def gelu(r, s, m):
                l = layer_of(s)
                c = l * M + m
                act.wait_ge(S["hid_done"], upto(r, s, M, m + 1))
                wait_room(act, r, s, m)
                act.activation(gh[:, m % 4], hid[:, m % 2], ACT.Gelu, bias=cols[:, c:c + 1])
                if m >= 2 or not (isinstance(r, int) and r == 0 and s == 0):
                    act.wait_ge(S["gl_ready"], upto(r, s, M, m - 1))
                act.activation(gt[:, m % 2], hid[:, m % 2], ACT.Gelu, bias=cols[:, c:c + 1]).then_inc(
                    S["gelu_done"], 1)

            def normalise(name, b, count):
                act.wait_ge(nb_ready[name], count)
                for t in range(T):
                    a = act.activation(u[:, b, t], u[:, b, t], ACT.Identity, bias=nb[name][:, t:t + 1],
                                       scale=rd[name][:, t:t + 1])
                a.then_inc(normed[name], 1)

            def slot(j):
                r = j.r

                def gelus(*ms):
                    if j.mlp is not None:
                        for m in ms:
                            gelu(r, j.mlp, m)

                gelus(1)
                if j.gat_wh is not None:
                    for k in range(KD):
                        act.wait_ge(S["ut_turned"], upto_gat(r, j.gat_wh, KD, k + 1))
                        act.activation(ut[:, k], big_k[:, k], ACT.Copy).then_inc(S["ut_ready"], 1)
                if j.mix is not None:
                    act.wait_ge(S["probs_turned"], upto(r, j.mix))
                    act.activation(pt[:, :, :], turn[:, :, :], ACT.Copy).then_inc(S["probs_ready"], 1)
                gelus(2)
                gelus(3)
                if j.gat_stats is not None:
                    normalise("u", buf_of(j.gat_stats), upto_gat(r, j.gat_stats))
                if j.gat_out is not None:
                    w = wh[:, buf_of(j.gat_out) % 2]
                    for h in range(2):
                        act.wait_ge(S["gmix_done"], upto_gat(r, j.gat_out, 2, h + 1))
                        act.activation(w[:, 2 * h:2 * h + 2], wide[:, 2 * h:2 * h + 2], ACT.Copy,
                                       scale=SLOPE).then_inc(S["gmix_scaled"], 1)
                gelus(4)
                if j.score is not None:
                    act.wait_ge(S["spread_done"], upto(r, j.score))
                    for t in range(T):
                        a = act.activation(sp[:, t], spread[:, t], ACT.Identity, bias=sc[:, t:t + 1])
                    a.then_inc(S["scores_sum"], 1)
                gelus(5)
                if j.mix is not None:
                    l = layer_of(j.mix)
                    for k in range(KD):
                        c = LAYERS * M + l * KD + k
                        cb = c + LAYERS * KD
                        act.wait_ge(S["z_turned"], upto(r, j.mix, KD, k + 1))
                        act.activation(hth[:, j.mix % 2, k], big_k[:, k], ACT.Identity, bias=cols[:, cb:cb + 1],
                                       scale=cols[:, c:c + 1])
                        act.activation(ht32[:, k], big_k[:, k], ACT.Identity, bias=cols[:, cb:cb + 1],
                                       scale=cols[:, c:c + 1]).then_inc(S["ht_ready"], 1)
                if j.gat_soft is not None:
                    act.wait_ge(S["gspread_done"], upto_gat(r, j.gat_soft))
                    for t in range(T):
                        a = act.activation(gsp[:, t], spread[:, t], ACT.Identity, bias=gsc[:, T + t:T + t + 1])
                    a.then_inc(S["gscores_sum"], 1)
                gelus(6)
                gelus(7)
                if j.gat_wh is not None:
                    if j.gat_out is not None:
                        act.wait_ge(S["out_added"], upto_gat(r, j.gat_out))
                    w = wh[:, buf_of(j.gat_wh) % 2]
                    for h in range(2):
                        act.wait_ge(S["wh_done"], upto_gat(r, j.gat_wh, 2, h + 1))
                        act.activation(w[:, 2 * h:2 * h + 2], wide[:, 2 * h:2 * h + 2], ACT.Copy).then_inc(
                            S["wh_ready"], 1)
                if j.mix is not None:
                    gelu(r, j.mix, 0)
                if j.gat_out is not None:
                    normalise("out", buf_of(j.gat_out), upto_gat(r, j.gat_out))
                if j.score is not None:
                    act.wait_ge(S["negmax"], upto(r, j.score))
                    for t in range(T):
                        a = act.activation(sp[:, t], sp[:, t], ACT.Exp, bias=nm[:, t:t + 1],
                                           accum_out=rs[:, t:t + 1])
                    a.then_inc(S["exp_done"], 1)
                if j.gat_soft is not None:
                    act.wait_ge(S["gnegmax"], upto_gat(r, j.gat_soft))
                    for t in range(T):
                        a = act.activation(gsp[:, t], gsp[:, t], ACT.Exp, bias=gnm[:, t:t + 1],
                                           accum_out=grs[:, t:t + 1])
                    a.then_inc(S["gexp_done"], 1)

            act.wait_ge(S["cols_ready"], 1)
            slots_of(act, slot)

        @block.tensor
        def _(pe):
            pe.wait_ge(S["ident_ready"], 2)
            pe.wait_ge(S["col_rows_in"], 16 * 3)
            pe.transpose(turn[:, 0, 0:NCOL], col_rows[:], ident[0:NCOL, 0:NCOL]).then_inc(S["cols_turned"], 1)
            pe.wait_ge(S["cols_ready"], 2)

            def mlp1(r, s, m):
                l, b = layer_of(s), s % 2
                if m == 0:
                    pe.wait_ge(S["htl_ready"], upto(r, s, KD))
                if m >= 2 or not (isinstance(r, int) and r == 0 and s == 0):
                    pe.wait_ge(S["gelu_done"], upto(r, s, M, m - 1))
                f = slice(m * P, (m + 1) * P)
                for k in range(KD):
                    pe.matmul(hid[:, m % 2], w1h[:, l, k, f], hth[:, b, k], start=(k == 0), stop=False)
                    pe.matmul(hid[:, m % 2], w1h[:, l, k, f], htl[:, b, k], start=False, stop=False)
                    a = pe.matmul(hid[:, m % 2], w1l[:, l, k, f], hth[:, b, k], start=False, stop=(k == KD - 1))
                a.then_inc(S["hid_done"], 1)

            def mlp2_part(s, m, tiles):
                l = layer_of(s)
                for t in tiles:
                    n = slice(t * P, (t + 1) * P)
                    pe.matmul(ff[:, t], gh[:, m % 4, n], w2h[:, l, m], start=(m == 0 and t % 2 == 0), stop=False,
                              skip_group_check=True)
                    pe.matmul(ff[:, t], gh[:, m % 4, n], w2l[:, l, m], start=False, stop=False,
                              skip_group_check=True)
                    a = pe.matmul(ff[:, t], gl[:, m % 4, n], w2h[:, l, m], start=False, stop=(m == M - 1),
                                  skip_group_check=True)
                return a

            def mlp2(r, s, m):
                pe.wait_ge(S["gl_ready"], upto(r, s, M, m + 1))
                if m == 0 and not (isinstance(r, int) and r == 0 and s == 0):
                    pe.wait_ge(S["ff_added"], upto(r, s - 1, 2))
                mlp2_part(s, m, range(T)).then_inc(S["mlp2_done"], 1)

            def mlp2_last(r, s, first):
                pe.wait_ge(S["gl_ready"], upto(r, s, M))
                for h in range(2):
                    for m in range(first, M):
                        a = mlp2_part(s, m, (2 * h, 2 * h + 1))
                        if h == 1 and m < M - 1:
                            a.then_inc(S["mlp2_done"], 1)
                    a.then_inc(S["ff_done"], 1)

            def slot(j):
                r = j.r
                before = Slot(r, j.s - 1, rounds)

                def first_half(*ms):
                    if j.mlp is not None:
                        for m in ms:
                            mlp1(r, j.mlp, m)

                def second_half(m):
                    if j.mlp is not None:
                        mlp2(r, j.mlp, m)

                def side_read():
                    if before.gat_wh is not None:
                        pe.wait_ge(S["wh_ready"], upto_gat(r, before.gat_wh, 2))
                    elif before.gat_soft is not None:
                        pe.wait_ge(S["gscores_sum"], upto_gat(r, before.gat_soft))
                        pe.wait_ge(S["ga_ready"], upto_gat(r, before.gat_soft))
                    elif before.score is not None:
                        pe.wait_ge(S["scores_sum"], upto(r, before.score))

                first_half(1)
                if j.gat_wh is not None:
                    b = buf_of(j.gat_wh)
                    pe.wait_ge(normed["u"], upto_gat(r, j.gat_wh))
                    if before.mix is not None:
                        pe.wait_ge(S["ht_ready"], upto(r, before.mix, KD))
                    elif before.gat_wh is not None:
                        pe.wait_ge(S["ut_ready"], upto_gat(r, before.gat_wh, KD))
                    for k in range(KD):
                        for t in range(T):
                            a = pe.transpose(big_k[:, k, t * P:(t + 1) * P], u[:, b, t, k * P:(k + 1) * P], ident[:])
                        a.then_inc(S["ut_turned"], 1)
                first_half(2)
                if j.mix is not None:
                    pe.wait_ge(S["exp_done"], upto(r, j.mix))
                    side_read()
                    for t in range(T):
                        a = pe.transpose(turn[:, t], sp[:, t], ident[:])
                    a.then_inc(S["probs_turned"], 1)
                second_half(0)
                first_half(3)
                if j.mix is not None:
                    b = buf_of(j.mix)
                    pe.wait_ge(S["probs_ready"], upto(r, j.mix))
                    if j.gat_wh is not None:
                        pe.wait_ge(S["ut_ready"], upto_gat(r, j.gat_wh, KD))
                    elif before.mix is not None:
                        pe.wait_ge(S["ht_ready"], upto(r, before.mix, KD))
                    for t in range(T):
                        a = pe.matmul(big_t[:, t], pt[:, t], xb[:, b, t], start=True, stop=True)
                        if t % 2:
                            a.then_inc(S["mix_done"], 1)
                first_half(4)
                second_half(1)
                if j.gat_out is not None:
                    pe.wait_ge(S["gprobs"], upto_gat(r, j.gat_out))
                    if j.mix is None:
                        side_read()
                    w = wh[:, buf_of(j.gat_out) % 2]
                    for t in range(T):
                        a = pe.matmul(wide[:, t], gsp[:, t], w[:, t], start=True, stop=True)
                        if t % 2:
                            a.then_inc(S["gmix_done"], 1)
                first_half(5)
                second_half(2)

                def side_read_again():
                    if j.gat_out is not None:
                        pe.wait_ge(S["gmix_leaky"], upto_gat(r, j.gat_out, 2))
                    elif j.mix is None:
                        side_read()

                if j.score is not None:
                    pe.wait_ge(S["scores_in"], upto(r, j.score, 2))
                    side_read_again()
                    for t in range(T):
                        a = pe.transpose(spread[:, t], sc[:, T + t:T + t + 1].broadcast_to([P, P]), ident[:])
                    a.then_inc(S["spread_done"], 1)
                if j.gat_soft is not None:
                    side_read_again()
                    pe.wait_ge(S["m01_ready"], upto_gat(r, j.gat_soft, per_tile))
                    for t in range(T):
                        a = pe.transpose(turn_b[:, t], m01[:, t], ident_b[:])
                    a.then_inc(S["masks_turned"], 1)
                if j.mix is not None:
                    b = buf_of(j.mix)
                    pe.wait_ge(normed["mix"], upto(r, j.mix))
                    for k in range(KD):
                        for t in range(T):
                            a = pe.transpose(big_k[:, k, t * P:(t + 1) * P], xb[:, b, t, k * P:(k + 1) * P], ident[:])
                        a.then_inc(S["z_turned"], 1)
                first_half(6)
                second_half(3)
                if j.gat_soft is not None:
                    pe.wait_ge(S["gscores_in"], upto_gat(r, j.gat_soft, 2))
                    if j.score is not None:
                        pe.wait_ge(S["scores_sum"], upto(r, j.score))
                    for t in range(T):
                        a = pe.transpose(spread[:, t], gsc[:, t:t + 1].broadcast_to([P, P]), ident[:])
                    a.then_inc(S["gspread_done"], 1)
                first_half(7)
                second_half(4)
                if j.gat_wh is not None:
                    pe.wait_ge(S["ut_ready"], upto_gat(r, j.gat_wh, KD))
                    if j.gat_soft is not None:
                        pe.wait_ge(S["gscores_sum"], upto_gat(r, j.gat_soft))
                        pe.wait_ge(S["ga_ready"], upto_gat(r, j.gat_soft))
                    elif j.score is not None:
                        pe.wait_ge(S["scores_sum"], upto(r, j.score))
                    else:
                        side_read_again()
                    for t in range(T):
                        for k in range(KD):
                            a = pe.matmul(wide[:, t], ut[:, k, t * P:(t + 1) * P], gw[:, k], start=(k == 0),
                                          stop=(k == KD - 1))
                        if t % 2:
                            a.then_inc(S["wh_done"], 1)
                second_half(5)
                if j.mix is not None:
                    mlp1(r, j.mix, 0)
                if j.mlp is not None:
                    mlp2_last(r, j.mlp, 6)

            pe.wait_ge(S["gw_in"], 32)
            slots_of(pe, slot)

        @block.vector
        def _(dve):
            dve.wait_ge(S["cols_turned"], 1)
            dve.tensor_copy(cols[:], turn[:, 0, 0:NCOL]).then_inc(S["cols_ready"], 1)
            dve.wait_ge(S["ident_ready"], 2)
            dve.tensor_copy(ident_b[:], ident[:]).then_inc(S["cols_ready"], 1)
            for a in range(per_tile):
                i = slice(a * nodes, (a + 1) * nodes)
                dve.tensor_copy(eye[i, :], ident[i, i]).then_inc(S["cols_ready"], 1)
            dve.wait_ge(S["cols_ready"], 2 + per_tile)
            dve.wait_ge(S["mask_ready0"], 2)
            dve.wait_ge(S["consts_ready"], 2)
            for a in range(per_tile):
                i = slice(a * nodes, (a + 1) * nodes)
                dve.memset(gat_off[i, i], GAT_OFF).then_inc(S["consts_ready"], 1)
            dve.wait_ge(S["rows_in"], 32)

            def wait_alone(s, count):
                dve.wait_ge(S["cols_ready"], 2)
                dve.wait_ge(s, count)

            def split_weight(w):
                l = w // 2
                hi, lo = ((w1h, w1l) if w % 2 == 0 else (w2h, w2l))
                dve.wait_ge(w_in[w % 2], 16 * (w // 2 + 1))
                dve.tensor_copy(hi[:, l], stage_view(w)).then_inc(S["split_hi"], 1)
                dve.wait_ge(S["split_hi"], w + 1)
                dve.tensor_tensor(lo[:, l], stage_view(w), hi[:, l].bitcast(F32), ALU.subtract).then_inc(
                    S["split_lo"], 1)

            def statistics(name, y, count, wait_tile):
                for t in range(T):
                    wait_tile(t)
                    a = dve.bn_stats(st[name][:, t], y[:, t])
                a.then_inc(stats_done[name], 1)
                wait_alone(stats_done[name], count)
                for t in range(T):
                    a = dve.bn_aggr(mv[name][:, t], st[name][:, t])
                a.then_inc(mean_done[name], 1)
                dve.wait_ge(mean_done[name], count)
                if name in nmean:
                    dve.tensor_scalar(nmean[name][:], mv[name][:, :, 0], -1.0, None, ALU.mult)
                dve.tensor_scalar(ve[name][:], mv[name][:, :, 1], EPS, None, ALU.add).then_inc(var_ready[name], 1)

            def normalise(name, y, count):
                dve.wait_ge(dev_ready[name], count)
                for t in range(T):
                    a = dve.tensor_scalar(y[:, t], y[:, t], mv[name][:, t, 0:1], rd[name][:, t:t + 1],
                                          ALU.subtract, ALU.mult)
                a.then_inc(normed[name], 1)

            def pair_scores(src, w_row, dst, bias, done, first_done, parts=(0, 1)):
                for c in parts:
                    if c == 1:
                        dve.wait_ge(done, first_done)
                    for t in range(T):
                        a = dve.tensor_tensor_reduce(unread[:, t], src[:, t], w_row[:, c * D:(c + 1) * D], 1.0,
                                                     bias if c == 0 else 0.0, ALU.mult, ALU.add,
                                                     dst[:, c * T + t:c * T + t + 1])
                    a.then_inc(done, 1)

            def slot(j):
                r = j.r

                def gl_part(*ms):
                    if j.mlp is not None:
                        for m in ms:
                            dve.wait_ge(S["gelu_done"], upto(r, j.mlp, M, m + 1))
                            wait_room(dve, r, j.mlp, m)
                            dve.tensor_tensor(gl[:, m % 4], gt[:, m % 2], gh[:, m % 4].bitcast(F32),
                                              ALU.subtract).then_inc(S["gl_ready"], 1)

                def next_pair_scores(*parts):
                    if j.pair is None:
                        return
                    b, l = buf_of(j.pair), layer_of(j.pair)
                    if 0 in parts:
                        if l == 0:
                            dve.wait_ge(x_in[b], r * 16 + 16 * (j.pair // ROUND + 1))
                        else:
                            dve.wait_ge(S["x_ready"], upto(r, j.pair - BUFS))
                        if j.score is not None:
                            dve.wait_ge(S["scores_sum"], upto(r, j.score))
                        before = Slot(r, j.s - 1, rounds)
                        if before.gat_wh is not None:
                            dve.wait_ge(S["gscores_in"], upto_gat(r, before.gat_wh, 2))
                    pair_scores(xb[:, b], score_w[:, l], sc, score_b[:, l:l + 1], S["scores_in"],
                                upto(r, j.pair, 2, 1), parts)

                if isinstance(r, int) and r == 0 and j.s in (-2, 0, 1):
                    w = 2 * max(j.s, -1) + 2
                    split_weight(w)
                    split_weight(w + 1)
                for h in range(2):
                    if j.norm is not None:
                        b = buf_of(j.norm)
                        if h == 0:
                            dve.wait_ge(S["h_ready"], upto(r, j.norm))
                        y = xb[:, b, 2 * h:2 * h + 2]
                        dve.wait_ge(S["ff_done"], upto(r, j.norm, 2, h + 1))
                        dve.tensor_tensor(y, ff[:, 2 * h:2 * h + 2], y, ALU.add).then_inc(S["ff_added"], 1)
                    if h == 0:
                        gl_part(0)
                if j.norm is not None:
                    statistics("mlp", xb[:, buf_of(j.norm)], upto(r, j.norm),
                               lambda t: dve.wait_ge(S["ff_added"], upto(r, j.norm, 2, t // 2 + 1)))
                if j.mix is not None:
                    dve.wait_ge(S["exp_done"], upto(r, j.mix))
                    dve.reciprocal(ri[:], rs[:]).then_inc(S["sum_inverse"], 1)
                if j.gat_out is not None:
                    dve.wait_ge(S["gexp_done"], upto_gat(r, j.gat_out))
                    dve.reciprocal(gri[:], grs[:]).then_inc(S["gsum_inverse"], 1)
                if j.gat_stats is not None:
                    dve.wait_ge(S["u_added"], upto_gat(r, j.gat_stats))
                    statistics("u", u[:, buf_of(j.gat_stats)], upto_gat(r, j.gat_stats), lambda t: None)
                gl_part(1)
                if j.norm is not None:
                    normalise("mlp", xb[:, buf_of(j.norm)], upto(r, j.norm))
                if j.mix is not None:
                    b = buf_of(j.mix)
                    dve.wait_ge(S["sum_inverse"], upto(r, j.mix))
                    for t in range(T):
                        if t % 2 == 0:
                            dve.wait_ge(S["mix_done"], upto(r, j.mix, 2, t // 2 + 1))
                        dve.scalar_tensor_tensor(out=xb[:, b, t], in0=big_t[:, t], scalar=ri[:, t:t + 1],
                                                 in1=xb[:, b, t], op0=ALU.mult, op1=ALU.add).then_inc(
                                                     S["mix_added"], 1)
                gl_part(2)
                if j.mix is not None:
                    statistics("mix", xb[:, buf_of(j.mix)], upto(r, j.mix),
                               lambda t: dve.wait_ge(S["mix_added"], upto(r, j.mix, T, t + 1)))
                gl_part(3)
                if j.mix is not None:
                    normalise("mix", xb[:, buf_of(j.mix)], upto(r, j.mix))
                if j.gat_out is not None:
                    for h in range(2):
                        dve.wait_ge(S["gmix_scaled"], upto_gat(r, j.gat_out, 2, h + 1))
                        w = wh[:, buf_of(j.gat_out) % 2, 2 * h:2 * h + 2]
                        dve.tensor_tensor(w, wide[:, 2 * h:2 * h + 2], w, ALU.max).then_inc(S["gmix_leaky"], 1)
                gl_part(4)
                if j.score is not None:
                    b = buf_of(j.score)
                    if layer_of(j.score) == 0:
                        dve.wait_ge(S["mask_ready"], upto_gat(r, j.score, per_tile))
                    dve.wait_ge(S["scores_sum"], upto(r, j.score))
                    dve.scalar_tensor_tensor(out=sp[:, :, :], in0=sp[:, :, :], scalar=SLOPE, in1=sp[:, :, :],
                                             op0=ALU.mult, op1=ALU.max).then_inc(S["scores_leaky"], 1)
                    wait_alone(S["scores_leaky"], upto(r, j.score))
                    for t in range(T):
                        a = dve.tensor_tensor_reduce(sp[:, t], sp[:, t], mask[:, b, t], 1.0, OFF, ALU.add, ALU.max,
                                                     mx[:, t:t + 1])
                    a.then_inc(S["max_done"], 1)
                    dve.wait_ge(S["max_done"], upto(r, j.score))
                    dve.tensor_scalar(nm[:], mx[:], -1.0, None, ALU.mult).then_inc(S["negmax"], 1)
                gl_part(5)
                if j.gat_soft is not None:
                    dve.wait_ge(S["masks_turned"], upto_gat(r, j.gat_soft))
                    dve.tensor_copy(gm[:, :, :], turn_b).then_inc(S["gm_ready"], 1)
                    dve.scalar_tensor_tensor(
                        out=ga[:, :, :], in0=turn_b, scalar=-GAT_OFF,
                        in1=gat_off[:].rearrange("p (o n) -> p o n", o=1).broadcast_to([P, T, P]),
                        op0=ALU.mult, op1=ALU.add).then_inc(S["ga_ready"], 1)
                    dve.wait_ge(S["gscores_sum"], upto_gat(r, j.gat_soft))
                    dve.scalar_tensor_tensor(out=gsp[:, :, :], in0=gsp[:, :, :], scalar=SLOPE, in1=gsp[:, :, :],
                                             op0=ALU.mult, op1=ALU.max).then_inc(S["gleaky"], 1)
                if j.gat_out is not None:
                    dve.wait_ge(S["out_added"], upto_gat(r, j.gat_out))
                    statistics("out", u[:, buf_of(j.gat_out)], upto_gat(r, j.gat_out), lambda t: None)
                if j.fresh is None:
                    next_pair_scores(0)
                gl_part(6)
                if j.gat_soft is not None:
                    wait_alone(S["gmasked"], upto_gat(r, j.gat_soft))
                    dve.wait_ge(S["ga_ready"], upto_gat(r, j.gat_soft))
                    for t in range(T):
                        a = dve.tensor_tensor_reduce(gsp[:, t], gsp[:, t], ga[:, t], 1.0, OFF, ALU.add, ALU.max,
                                                     gmx[:, t:t + 1])
                    a.then_inc(S["gmax_done"], 1)
                    dve.wait_ge(S["gmax_done"], upto_gat(r, j.gat_soft))
                    dve.tensor_scalar(gnm[:], gmx[:], -1.0, None, ALU.mult).then_inc(S["gnegmax"], 1)
                if j.fresh is not None:
                    b = buf_of(j.fresh)
                    dve.wait_ge(S["adj_a_in"], upto_gat(r, j.fresh, 16))
                    dve.tensor_tensor(adj_e[:], adj_a[:], eye[:].rearrange("p (o j) -> p o j", o=1).broadcast_to(
                        [P, T, nodes]), ALU.add).then_inc(S["mask_edges"], 1)
                    dve.wait_ge(S["mask_edges"], upto_gat(r, j.fresh))
                    for a in range(per_tile):
                        i = slice(a * nodes, (a + 1) * nodes)
                        dve.tensor_scalar(mask[i, b, :, i], adj_e[i], 0.0, OFF, ALU.is_le, ALU.mult).then_inc(
                            S["mask_ready"], 1)
                if j.gat_wh is not None:
                    dve.wait_ge(S["adj_t_in"], upto_gat(r, j.gat_wh, 16))
                    if j.gat_soft is not None:
                        dve.wait_ge(S["gmasked"], upto_gat(r, j.gat_soft))
                    for a in range(per_tile):
                        i = slice(a * nodes, (a + 1) * nodes)
                        dve.tensor_scalar(m01[i, :, i], adj_t[i], 0.0, None, ALU.is_gt).then_inc(S["m01_ready"], 1)
                gl_part(7)
                next_pair_scores(*((1,) if j.fresh is None else (0, 1)))
                if j.gat_wh is not None:
                    w = wh[:, buf_of(j.gat_wh) % 2]
                    dve.wait_ge(S["wh_ready"], upto_gat(r, j.gat_wh, 2))
                    if j.pair is not None:
                        dve.wait_ge(S["scores_in"], upto(r, j.pair, 2))
                    pair_scores(w, gat_w[:], gsc, 0.0, S["gscores_in"], upto_gat(r, j.gat_wh, 2, 1))

            slots_of(dve, slot)


_INS = ['x', 'adj', 'L0_gnn_attn_w', 'L0_gnn_attn_b', 'L0_gnn_W1', 'L0_gnn_b1', 'L0_gnn_W2', 'L0_gnn_b2',
        'L0_gnn_g1', 'L0_gnn_beta1', 'L0_gnn_g2', 'L0_gnn_beta2', 'L1_gnn_W', 'L1_gnn_a']


def kernel(**inputs):
    import numpy as _np
    import concourse.bacc as _bacc
    from concourse import mybir as _mybir
    from concourse.bass_utils import run_bass_kernel_spmd as _run

    nc = _bacc.Bacc("TRN2", target_bir_lowering=False, num_devices=1, dynamic_dma_scratch_size=1024)
    arrays, args = {}, []
    for name in _INS:
        a = _np.ascontiguousarray(inputs[name])
        arrays[f"in_{name}_dram"] = a
        args.append(nc.dram_tensor(f"in_{name}_dram", a.shape, _mybir.dt.from_np(a.dtype), kind="ExternalInput").ap())
    shape = tuple(inputs['x'].shape)
    args.append(nc.dram_tensor("out_0_dram", shape, _mybir.dt.float32, kind="ExternalOutput").ap())
    graph_net_kernel(nc, *args)
    r = _run(nc, [arrays], core_ids=[0])
    return r.results[0]["out_0_dram"]
```

```python
from contextlib import ExitStack

import concourse.bass as bass
from concourse import mybir

F32 = mybir.dt.float32
F32R = mybir.dt.float32r
BF16 = mybir.dt.bfloat16
I32 = mybir.dt.int32
ALU = mybir.AluOpType
ACT = mybir.ActivationFunctionType

P = 128
T = 4
BUFS = 4
LAYERS = 3
ROUND = BUFS * LAYERS
FIRST = 5
EPS = 1e-5
SLOPE = 0.2
OFF = -3.0e38
GAT_OFF = -9.0e15


def layer_of(s):
    return (s % ROUND) // BUFS


def buf_of(s):
    return s % BUFS


def group_of(r, s):
    return r * BUFS + (BUFS * (s // ROUND) + s % BUFS)


def upto(r, s, per=1, part=None):
    return r * (ROUND * per) + (s * per + (per if part is None else part))


def upto_gat(r, s, per=1, part=None):
    return r * (BUFS * per) + ((BUFS * (s // ROUND) + s % BUFS) * per + (per if part is None else part))


class Slot:

    def __init__(self, r, s, rounds):
        q = (r if isinstance(r, int) else 1) * ROUND + s
        jobs = rounds * ROUND
        self.r, self.s = r, s
        self.tail = q >= jobs
        self.mlp = s if 0 <= q < jobs else None
        self.norm = s - 1 if 0 <= q - 1 < jobs else None
        self.pair = s + 3 if 0 <= q + 3 < jobs else None
        self.score = s + 2 if 0 <= q + 2 < jobs else None
        self.mix = s + 1 if 0 <= q + 1 < jobs else None

        def last_layer(d):
            return s - d if 0 <= q - d < jobs and layer_of(s - d) == LAYERS - 1 else None

        self.gat_in = last_layer(0)
        self.gat_sum = last_layer(1)
        self.gat_stats = last_layer(2)
        self.gat_wh = last_layer(3)
        self.gat_soft = last_layer(4)
        self.gat_out = last_layer(5)
        self.fresh = self.pair if self.pair is not None and layer_of(self.pair) == 0 else None


def graph_net_kernel(nc, x, adj, attn_w, attn_b, W1, b1, W2, b2, g1, beta1, g2, beta2, gat_W, gat_a, out):
    graphs, nodes, D = x.shape
    F = W1.shape[2]
    KD = D // P
    M = F // P
    per_tile = P // nodes
    groups = graphs // (per_tile * T)
    rounds = groups // BUFS
    NT = T * P
    assert groups % BUFS == 0 and nodes * per_tile == P and D * 2 == NT

    x_g = x.rearrange("(G t g) i d -> G (g i) t d", t=T, g=per_tile)
    adj_g = adj.rearrange("(G t g) i j -> G (g i) t j", t=T, g=per_tile)
    out_g = out.rearrange("(G t g) i d -> G (g i) t d", t=T, g=per_tile)

    with ExitStack() as ctx:
        def sb(name, shape, dt=F32):
            return ctx.enter_context(nc.sbuf_tensor(name, shape, dt))

        def ps(name, shape, dt=F32):
            return ctx.enter_context(nc.psum_tensor(name, shape, dt))

        def sem(name):
            return ctx.enter_context(nc.semaphore(name))

        w1h = sb("w1h", [P, LAYERS, KD, F], F32R)
        w1l = sb("w1l", [P, LAYERS, KD, F], F32R)
        w2h = sb("w2h", [P, LAYERS, M, D], F32R)
        w2l = sb("w2l", [P, LAYERS, M, D], F32R)
        gw = sb("gw", [P, KD, D])
        NCOL = LAYERS * (M + 2 * KD)
        cols = sb("cols", [P, NCOL])
        score_w = sb("score_w", [P, LAYERS, 2 * D])
        gat_w = sb("gat_w", [P, 2 * D])
        score_b = sb("score_b", [P, LAYERS])
        g1_row = sb("g1_row", [P, LAYERS, D])
        hb_row = sb("hb_row", [P, LAYERS, D])
        g2_row = sb("g2_row", [P, LAYERS, D])
        be2_row = sb("be2_row", [P, LAYERS, D])
        ident = sb("ident", [P, P])
        ident_b = sb("ident_b", [P, P], BF16)
        eye = sb("eye", [P, nodes])
        gat_off = sb("gat_off", [P, P])
        half = sb("half", [P, T])
        xb = sb("xb", [P, BUFS, T, D])
        ht32 = sb("ht32", [P, KD, NT])
        hth = sb("hth", [P, 2, KD, NT], F32R)
        htl = sb("htl", [P, 2, KD, NT], F32R)
        gt = sb("gt", [P, 2, NT])
        gh = sb("gh", [P, 4, NT], F32R)
        gl = sb("gl", [P, 4, NT], F32R)
        adj_a = sb("adj_a", [P, T, nodes], I32)
        adj_e = sb("adj_e", [P, T, nodes], BF16)
        mask = sb("mask", [P, BUFS, T, P], BF16)
        sc = sb("sc", [P, 2, 2 * T])
        sp = sb("sp", [P, T, P])
        pt = sb("pt", [P, T, P])
        unread = sb("unread", [P, T, D], BF16)
        mx = sb("mx", [P, T])
        nm = sb("nm", [P, T])
        rs = sb("rs", [P, T])
        ri = sb("ri", [P, T])
        norm_names = ("mix", "mlp", "u", "out")
        st = {n: sb(f"st_{n}", [P, T, 6]) for n in norm_names}
        mv = {n: sb(f"mv_{n}", [P, T, 2]) for n in norm_names}
        ve = {n: sb(f"ve_{n}", [P, T]) for n in norm_names}
        rd = {n: sb(f"rd_{n}", [P, T]) for n in norm_names}
        nmean = {n: sb(f"nmean_{n}", [P, T]) for n in ("u", "out")}
        nb = {n: sb(f"nb_{n}", [P, T]) for n in ("u", "out")}
        u = sb("u", [P, BUFS, T, D])
        wh = sb("wh", [P, 2, T, D])
        ut = sb("ut", [P, KD, NT])
        adj_t = sb("adj_t", [P, T, nodes], I32)
        col_rows = adj_t[0:NCOL, :, :].rearrange("p t n -> p (t n)").bitcast(F32)[:, 0:P]
        m01 = sb("m01", [P, T, P], BF16)
        gm = m01
        ga = sb("ga", [P, T, P])
        gsc = sb("gsc", [P, 2 * T])
        gsp = sb("gsp", [P, T, P])
        gmx = sb("gmx", [P, T])
        gnm = sb("gnm", [P, T])
        grs = sb("grs", [P, T])
        gri = sb("gri", [P, T])
        stage = [u[:, 0:2, :, :].rearrange("p a t d -> p (a t d)"), wh[:, :, :, :].rearrange("p a t d -> p (a t d)")]
        beta_tmp = u[:, 2, 0:LAYERS, :]

        hid = ps("hid", [P, 2, NT])
        ff = ps("ff", [P, T, D])
        big = ps("big", [P, T * D])
        side = ps("side", [P, 2, T, P])
        spread = side[:, 0]
        turn = side[:, 1]
        wide = side[:, :, :, :].rearrange("p a t n -> p (a t n)").rearrange("p (t d) -> p t d", t=T)
        big_t = big[:, :].rearrange("p (t d) -> p t d", t=T)
        big_k = big[:, :].rearrange("p (k n) -> p k n", k=KD)
        turn_b = turn.rearrange("p t n -> p (t n)").bitcast(BF16)[:, 0:T * P].rearrange("p (t n) -> p t n", t=T)

        names = """table_ready col_rows_in rows_in more_rows_in beta_in gain_in gw_in
            adj_a_in adj_t_in ident_ready consts_ready mask_ready0 cols_turned cols_ready hb_ready
            split_hi split_lo mask_edges mask_ready
            scores_in spread_done scores_sum scores_leaky max_done negmax exp_done probs_turned
            probs_ready sum_inverse mix_done mix_added z_turned ht_ready htl_ready h_scaled h_ready
            hid_done gelu_done gl_ready mlp2_done ff_done ff_added x_scaled x_ready
            u_part u_added ut_turned ut_ready wh_done wh_ready m01_ready masks_turned gm_ready ga_ready
            gscores_in gspread_done gscores_sum gleaky gmasked gmax_done gnegmax gexp_done gsum_inverse
            gprobs gmix_done gmix_scaled gmix_leaky out_added""".split()
        S = {n: sem(n) for n in names}
        x_in = [sem(f"x_in{i}") for i in range(BUFS)]
        w_in = [sem(f"w_in{i}") for i in range(2)]
        u_in = [sem(f"u_in{i}") for i in range(BUFS)]
        out_in = [sem(f"out_stored{i}") for i in range(BUFS)]
        stats_done = {n: sem(f"stats_{n}") for n in norm_names}
        mean_done = {n: sem(f"mean_{n}") for n in norm_names}
        var_ready = {n: sem(f"var_{n}") for n in norm_names}
        dev_ready = {n: sem(f"dev_{n}") for n in norm_names}
        nb_ready = {n: sem(f"nb_{n}_ready") for n in ("u", "out")}
        normed = {n: sem(f"normed_{n}") for n in norm_names}

        N_SPLITS = 2 * LAYERS

        def raw_weight(w):
            l = w // 2
            return (W1[l].rearrange("(k p) f -> p k f", p=P) if w % 2 == 0
                    else W2[l].rearrange("(m p) d -> p m d", p=P))

        def stage_view(w):
            return stage[w % 2].rearrange("p (a b) -> p a b", a=KD if w % 2 == 0 else M)

        def slots_of(engine, slot):
            for s in range(-3, FIRST):
                slot(Slot(0, s, rounds))
            with engine.Fori(0, rounds - 1) as r:
                for s in range(FIRST, FIRST + ROUND):
                    slot(Slot(r, s, rounds))
            for s in range(FIRST, FIRST + ROUND):
                slot(Slot(rounds - 1, s, rounds))

        def wait_room(eng, r, s, m):
            if m >= 4:
                eng.wait_ge(S["mlp2_done"], upto(r, s, M - 1, m - 3))
            elif isinstance(r, int) and r == 0 and s == 0:
                return
            elif m < 3:
                eng.wait_ge(S["mlp2_done"], upto(r, s - 1, M - 1, m + 5))
            else:
                eng.wait_ge(S["ff_done"], upto(r, s - 1, 2))


        def gat_mix(j):
            return ff if j.tail else wide

        def mix_room(j):
            if j.tail:
                return ht32[:, :, :].rearrange("p k n -> p (k n)").rearrange("p (t d) -> p t d", t=T)
            return wh[:, buf_of(j.gat_out) % 2]

        def wh_banks(j):
            return big_t if j.tail else wide

        def gat_scores(j, s):
            return sp if isinstance(j.r, int) and s % 2 else gsp

        block = ctx.enter_context(nc.Block())

        @block.sync
        def _(sp_eng):
            def load_x(r, b):
                g = r * BUFS + b
                sp_eng.dma_start(xb[:, b], x_g[g]).then_inc(x_in[b], 16)

            def load_weight(w):
                if w >= 2:
                    sp_eng.wait_ge(S["split_lo"], w - 1)
                sp_eng.dma_start(stage_view(w), raw_weight(w)).then_inc(w_in[w % 2], 16)

            sp_eng.dma_start(col_rows[0:LAYERS * M], b1.rearrange("l (m p) -> (l m) p", p=P)).then_inc(
                S["col_rows_in"], 16)
            o = LAYERS * M
            for v in (g1, beta1):
                sp_eng.dma_start(col_rows[o:o + LAYERS * KD], v.rearrange("l (k p) -> (l k) p", p=P)).then_inc(
                    S["col_rows_in"], 16)
                o += LAYERS * KD
            load_x(0, 0)
            sp_eng.dma_start(adj_a[:], adj_g[0]).then_inc(S["adj_a_in"], 16)

            def row(v, n):
                return v.rearrange("(o l) d -> o (l d)", o=1).broadcast_to([P, n])

            def flat(t):
                return t[:, :, :].rearrange("p l d -> p (l d)")

            sp_eng.dma_start(score_w[:, 0], row(attn_w[0:1], 2 * D)).then_inc(S["rows_in"], 16)
            sp_eng.dma_start(score_b[:], attn_b.rearrange("(o l) -> o l", o=1).broadcast_to([P, LAYERS])).then_inc(
                S["rows_in"], 16)
            load_x(0, 1)
            load_weight(0)

            def later_loads(step):
                if step == 0:
                    sp_eng.dma_start(score_w[:, 1:LAYERS, :].rearrange("p l d -> p (l d)"),
                                     row(attn_w[1:LAYERS], (LAYERS - 1) * 2 * D)).then_inc(S["more_rows_in"], 16)
                    sp_eng.dma_start(flat(hb_row), row(beta1, LAYERS * D)).then_inc(S["beta_in"], 16)
                    sp_eng.dma_start(flat(beta_tmp), row(b2, LAYERS * D)).then_inc(S["beta_in"], 16)
                    sp_eng.dma_start(flat(g1_row), row(g1, LAYERS * D)).then_inc(S["beta_in"], 16)
                    load_weight(1)
                    load_x(0, 2)
                    sp_eng.dma_start(flat(g2_row), row(g2, LAYERS * D)).then_inc(S["gain_in"], 16)
                    sp_eng.dma_start(flat(be2_row), row(beta2, LAYERS * D)).then_inc(S["gain_in"], 16)
                elif step == 1:
                    load_x(0, 3)
                    sp_eng.wait_ge(S["cols_turned"], 1)
                    sp_eng.dma_start(adj_t[:], adj_g[0]).then_inc(S["adj_t_in"], 16)
                    sp_eng.dma_start(gat_w[:], gat_a.rearrange("(o d) c -> o (d c)", o=1).broadcast_to(
                        [P, 2 * D])).then_inc(S["gw_in"], 16)
                    sp_eng.dma_start(gw[:], gat_W.rearrange("(k p) d -> p k d", p=P)).then_inc(S["gw_in"], 16)

            for o_sem in out_in:
                sp_eng.sem_inc(o_sem, 16)

            def slot(j):
                r = j.r
                if isinstance(r, int) and r == 0 and j.s == FIRST - 1:
                    sp_eng.wait_ge(S["split_lo"], N_SPLITS)
                    sp_eng.wait_ge(S["hb_ready"], 1)
                if j.fresh:
                    sp_eng.wait_ge(S["mask_edges"], upto_gat(r, j.fresh - 1))
                    sp_eng.dma_start(adj_a[:], adj_g[group_of(r, j.fresh)]).then_inc(S["adj_a_in"], 16)
                if isinstance(r, int) and r == 0 and j.s in (-2, -1):
                    later_loads(j.s + 2)
                if isinstance(r, int) and r == 0 and -1 <= j.s < N_SPLITS - 3:
                    load_weight(j.s + 3)
                if j.gat_in is not None:
                    b = buf_of(j.gat_in)
                    sp_eng.wait_ge(out_in[b], r * 16 + 16)
                    sp_eng.dma_start(u[:, b], x_g[group_of(r, j.gat_in)]).then_inc(u_in[b], 16)
                if j.gat_sum is not None and not (isinstance(r, int) and group_of(r, j.gat_sum) + BUFS >= groups):
                    sp_eng.wait_ge(S["u_added"], upto_gat(r, j.gat_sum))
                    load_x(r + 1, buf_of(j.gat_sum))
                if j.gat_wh is not None and not (isinstance(r, int) and group_of(r, j.gat_wh) + 1 >= groups):
                    sp_eng.wait_ge(S["m01_ready"], upto_gat(r, j.gat_wh, per_tile))
                    sp_eng.dma_start(adj_t[:], adj_g[group_of(r, j.gat_wh) + 1]).then_inc(S["adj_t_in"], 16)
                if j.gat_out is not None:
                    b = buf_of(j.gat_out)
                    sp_eng.wait_ge(normed["out"], upto_gat(r, j.gat_out))
                    sp_eng.dma_start(out_g[group_of(r, j.gat_out)], u[:, b]).then_inc(out_in[b], 16)

            slots_of(sp_eng, slot)
            for o_sem in out_in:
                sp_eng.wait_ge(o_sem, 16 * (rounds + 1))

        @block.gpsimd
        def _(pool):
            pool.memset(ident[:], 0.0).then_inc(S["ident_ready"], 1)
            pool.memset(half[:], -0.5).then_inc(S["consts_ready"], 1)
            pool.memset(mask[:, :, :, :], OFF).then_inc(S["mask_ready0"], 1)
            pool.wait_ge(S["ident_ready"], 1)
            pool.affine_select(out=ident[:], in_=ident[:], compare_op=ALU.not_equal, fill=1.0, base=0,
                               pattern=[[-1, P]], channel_multiplier=1).then_inc(S["ident_ready"], 1)
            pool.memset(m01[:, :, :], 0.0).then_inc(S["mask_ready0"], 1)
            pool.memset(gat_off[:], OFF).then_inc(S["consts_ready"], 1)
            pool.wait_ge(S["consts_ready"], 2)
            pool.wait_ge(S["beta_in"], 16 * 3)
            pool.tensor_tensor(hb_row[:], hb_row[:], beta_tmp, ALU.add).then_inc(S["hb_ready"], 1)
            pool.wait_ge(S["hb_ready"], 1)

            def power(name, count):
                pool.wait_ge(var_ready[name], count)
                pool.tensor_tensor(rd[name][:], ve[name][:], half[:], ALU.pow).then_inc(dev_ready[name], 1)

            def gain_mult(s, gain, scaled):
                b, l = buf_of(s), layer_of(s)
                pool.tensor_tensor(xb[:, b], xb[:, b], gain[:, l:l + 1, :].broadcast_to([P, T, D]),
                                   ALU.mult).then_inc(scaled, 1)

            def gain_add(r, s, bias, scaled, ready):
                b, l = buf_of(s), layer_of(s)
                pool.wait_ge(scaled, upto(r, s))
                pool.tensor_tensor(xb[:, b], xb[:, b], bias[:, l:l + 1, :].broadcast_to([P, T, D]),
                                   ALU.add).then_inc(ready, 1)

            def power_and_shift(name, count):
                power(name, count)
                pool.wait_ge(dev_ready[name], count)
                pool.tensor_tensor(nb[name][:], nmean[name][:], rd[name][:], ALU.mult).then_inc(nb_ready[name], 1)

            def slot(j):
                r = j.r

                def gat_probabilities(job):
                    if job is None:
                        return
                    pool.wait_ge(S["gsum_inverse"], upto_gat(r, job))
                    g = gat_scores(j, job)
                    pool.tensor_tensor(g[:, :, :], g[:, :, :], gri[:].rearrange("p (t o) -> p t o", o=1).broadcast_to(
                        [P, T, P]), ALU.mult).then_inc(S["gprobs"], 1)

                def mlp_deviation():
                    if j.norm is None:
                        return
                    power("mlp", upto(r, j.norm))

                def u_deviation():
                    if j.gat_stats is None:
                        return
                    power_and_shift("u", upto_gat(r, j.gat_stats))

                def mlp_gain():
                    if j.norm is None:
                        return
                    pool.wait_ge(normed["mlp"], upto(r, j.norm))
                    gain_mult(j.norm, g2_row, S["x_scaled"])

                def mlp_bias():
                    if j.norm is None:
                        return
                    gain_add(r, j.norm, be2_row, S["x_scaled"], S["x_ready"])

                def out_sum():
                    if j.gat_out is None:
                        return
                    b = buf_of(j.gat_out)
                    pool.wait_ge(S["gmix_leaky"], upto_gat(r, j.gat_out, 2))
                    pool.tensor_tensor(u[:, b], u[:, b], mix_room(j), ALU.add).then_inc(S["out_added"], 1)

                def u_sum():
                    if j.gat_sum is None:
                        return
                    b = buf_of(j.gat_sum)
                    pool.wait_ge(S["x_ready"], upto(r, j.gat_sum))
                    pool.wait_ge(u_in[b], r * 16 + 16)
                    pool.tensor_tensor(u[:, b], u[:, b], xb[:, b], ALU.add).then_inc(S["u_added"], 1)

                def out_deviation():
                    if j.gat_out is None:
                        return
                    power_and_shift("out", upto_gat(r, j.gat_out))

                def gat_mask():
                    if j.gat_soft is None:
                        return
                    pool.wait_ge(S["gleaky"], upto_gat(r, j.gat_soft))
                    pool.wait_ge(S["gm_ready"], upto_gat(r, j.gat_soft))
                    g = gat_scores(j, j.gat_soft)
                    pool.tensor_tensor(g[:, :, :], g[:, :, :], gm[:, :, :], ALU.mult).then_inc(S["gmasked"], 1)

                if j.tail:
                    mlp_deviation()
                    gat_mask()
                    u_deviation()
                    mlp_gain()
                    mlp_bias()
                    out_sum()
                    gat_probabilities(j.gat_soft)
                    u_sum()
                    out_deviation()
                    return
                gat_probabilities(j.gat_out)
                mlp_deviation()
                if isinstance(r, int) and r == 0 and j.s == 1:
                    pool.wait_ge(S["gain_in"], 16 * 2)
                mlp_gain()
                if j.mix is not None:
                    power("mix", upto(r, j.mix))
                mlp_bias()
                out_sum()
                u_sum()
                if j.mix is not None:
                    for k in range(KD):
                        pool.wait_ge(S["ht_ready"], upto(r, j.mix, KD, k + 1))
                        pool.tensor_tensor(htl[:, j.mix % 2, k], ht32[:, k], hth[:, j.mix % 2, k].bitcast(F32),
                                           ALU.subtract).then_inc(S["htl_ready"], 1)
                u_deviation()
                out_deviation()
                gat_mask()
                if j.mix is not None:
                    pool.wait_ge(S["z_turned"], upto(r, j.mix, KD))
                    gain_mult(j.mix, g1_row, S["h_scaled"])
                    gain_add(r, j.mix, hb_row, S["h_scaled"], S["h_ready"])

            slots_of(pool, slot)

        @block.scalar
        def _(act):
            def gelu(r, s, m):
                l = layer_of(s)
                c = l * M + m
                act.wait_ge(S["hid_done"], upto(r, s, M, m + 1))
                wait_room(act, r, s, m)
                act.activation(gh[:, m % 4], hid[:, m % 2], ACT.Gelu, bias=cols[:, c:c + 1])
                if m >= 2 or not (isinstance(r, int) and r == 0 and s == 0):
                    act.wait_ge(S["gl_ready"], upto(r, s, M, m - 1))
                act.activation(gt[:, m % 2], hid[:, m % 2], ACT.Gelu, bias=cols[:, c:c + 1]).then_inc(
                    S["gelu_done"], 1)

            def normalise(name, b, count):
                act.wait_ge(nb_ready[name], count)
                for t in range(T):
                    a = act.activation(u[:, b, t], u[:, b, t], ACT.Identity, bias=nb[name][:, t:t + 1],
                                       scale=rd[name][:, t:t + 1])
                a.then_inc(normed[name], 1)

            def slot(j):
                r = j.r

                def gelus(*ms):
                    if j.mlp is not None:
                        for m in ms:
                            gelu(r, j.mlp, m)

                def ut_out():
                    if j.gat_wh is None:
                        return
                    for k in range(KD):
                        act.wait_ge(S["ut_turned"], upto_gat(r, j.gat_wh, KD, k + 1))
                        act.activation(ut[:, k], big_k[:, k], ACT.Copy).then_inc(S["ut_ready"], 1)

                def u_norm():
                    if j.gat_stats is None:
                        return
                    normalise("u", buf_of(j.gat_stats), upto_gat(r, j.gat_stats))

                def gat_scaled():
                    if j.gat_out is None:
                        return
                    w = mix_room(j)
                    for h in range(2):
                        act.wait_ge(S["gmix_done"], upto_gat(r, j.gat_out, 2, h + 1))
                        act.activation(w[:, 2 * h:2 * h + 2], gat_mix(j)[:, 2 * h:2 * h + 2], ACT.Copy,
                                       scale=SLOPE).then_inc(S["gmix_scaled"], 1)

                def gat_sums():
                    if j.gat_soft is None:
                        return
                    act.wait_ge(S["gspread_done"], upto_gat(r, j.gat_soft))
                    for t in range(T):
                        a = act.activation(gat_scores(j, j.gat_soft)[:, t], spread[:, t], ACT.Identity,
                                           bias=gsc[:, T + t:T + t + 1])
                    a.then_inc(S["gscores_sum"], 1)

                def wh_out():
                    if j.gat_wh is None:
                        return
                    if j.gat_out is not None and j.tail:
                        act.wait_ge(S["gmix_done"], upto_gat(r, j.gat_out, 2))
                    elif j.gat_out is not None:
                        act.wait_ge(S["out_added"], upto_gat(r, j.gat_out))
                    w = wh[:, buf_of(j.gat_wh) % 2]
                    for h in range(2):
                        act.wait_ge(S["wh_done"], upto_gat(r, j.gat_wh, 2, h + 1))
                        act.activation(w[:, 2 * h:2 * h + 2], wh_banks(j)[:, 2 * h:2 * h + 2], ACT.Copy).then_inc(
                            S["wh_ready"], 1)

                def out_norm(job):
                    if job is None:
                        return
                    normalise("out", buf_of(job), upto_gat(r, job))

                def gat_exp():
                    if j.gat_soft is None:
                        return
                    act.wait_ge(S["gnegmax"], upto_gat(r, j.gat_soft))
                    g = gat_scores(j, j.gat_soft)
                    for t in range(T):
                        a = act.activation(g[:, t], g[:, t], ACT.Exp, bias=gnm[:, t:t + 1],
                                           accum_out=grs[:, t:t + 1])
                    a.then_inc(S["gexp_done"], 1)

                if j.tail:
                    ut_out()
                    gat_sums()
                    before = Slot(r, j.s - 1, rounds)
                    if before.tail:
                        out_norm(before.gat_out)
                    gat_scaled()
                    wh_out()
                    u_norm()
                    gat_exp()
                    if j.s == FIRST + ROUND - 1:
                        out_norm(j.gat_out)
                    return
                gelus(1)
                ut_out()
                if j.mix is not None:
                    act.wait_ge(S["probs_turned"], upto(r, j.mix))
                    act.activation(pt[:, :, :], turn[:, :, :], ACT.Copy).then_inc(S["probs_ready"], 1)
                gelus(2)
                gelus(3)
                gat_scaled()
                gelus(4)
                gelus(5)
                if j.mix is not None:
                    l = layer_of(j.mix)
                    for k in range(KD):
                        c = LAYERS * M + l * KD + k
                        cb = c + LAYERS * KD
                        act.wait_ge(S["z_turned"], upto(r, j.mix, KD, k + 1))
                        act.activation(hth[:, j.mix % 2, k], big_k[:, k], ACT.Identity, bias=cols[:, cb:cb + 1],
                                       scale=cols[:, c:c + 1])
                        act.activation(ht32[:, k], big_k[:, k], ACT.Identity, bias=cols[:, cb:cb + 1],
                                       scale=cols[:, c:c + 1]).then_inc(S["ht_ready"], 1)
                if j.score is not None:
                    act.wait_ge(S["spread_done"], upto(r, j.score))
                    for t in range(T):
                        a = act.activation(sp[:, t], spread[:, t], ACT.Identity, bias=sc[:, j.score % 2, t:t + 1])
                    a.then_inc(S["scores_sum"], 1)
                gelus(6)
                gat_sums()
                gelus(7)
                u_norm()
                out_norm(j.gat_out)
                if j.mix is not None:
                    gelu(r, j.mix, 0)
                wh_out()
                if j.score is not None:
                    act.wait_ge(S["negmax"], upto(r, j.score))
                    for t in range(T):
                        a = act.activation(sp[:, t], sp[:, t], ACT.Exp, bias=nm[:, t:t + 1],
                                           accum_out=rs[:, t:t + 1])
                    a.then_inc(S["exp_done"], 1)
                gat_exp()

            act.wait_ge(S["cols_ready"], 1)
            act.wait_ge(S["consts_ready"], 2)
            act.activation(grs[:], half[:], ACT.Exp).then_inc(S["table_ready"], 1)
            slots_of(act, slot)

        @block.tensor
        def _(pe):
            pe.wait_ge(S["ident_ready"], 2)
            pe.wait_ge(S["col_rows_in"], 16 * 3)
            pe.transpose(turn[:, 0, 0:NCOL], col_rows[:], ident[0:NCOL, 0:NCOL]).then_inc(S["cols_turned"], 1)
            pe.wait_ge(S["cols_ready"], 2)

            def mlp1(r, s, m):
                l, b = layer_of(s), s % 2
                if m == 0:
                    pe.wait_ge(S["htl_ready"], upto(r, s, KD))
                if m >= 2 or not (isinstance(r, int) and r == 0 and s == 0):
                    pe.wait_ge(S["gelu_done"], upto(r, s, M, m - 1))
                f = slice(m * P, (m + 1) * P)
                for k in range(KD):
                    pe.matmul(hid[:, m % 2], w1h[:, l, k, f], hth[:, b, k], start=(k == 0), stop=False)
                    pe.matmul(hid[:, m % 2], w1h[:, l, k, f], htl[:, b, k], start=False, stop=False)
                    a = pe.matmul(hid[:, m % 2], w1l[:, l, k, f], hth[:, b, k], start=False, stop=(k == KD - 1))
                a.then_inc(S["hid_done"], 1)

            def mlp2_part(s, m, tiles):
                l = layer_of(s)
                for t in tiles:
                    n = slice(t * P, (t + 1) * P)
                    pe.matmul(ff[:, t], gh[:, m % 4, n], w2h[:, l, m], start=(m == 0 and t % 2 == 0), stop=False,
                              skip_group_check=True)
                    pe.matmul(ff[:, t], gh[:, m % 4, n], w2l[:, l, m], start=False, stop=False,
                              skip_group_check=True)
                    a = pe.matmul(ff[:, t], gl[:, m % 4, n], w2h[:, l, m], start=False, stop=(m == M - 1),
                                  skip_group_check=True)
                return a

            def mlp2(r, s, m):
                pe.wait_ge(S["gl_ready"], upto(r, s, M, m + 1))
                if m == 0 and not (isinstance(r, int) and r == 0 and s == 0):
                    pe.wait_ge(S["ff_added"], upto(r, s - 1, 2))
                mlp2_part(s, m, range(T)).then_inc(S["mlp2_done"], 1)

            def mlp2_last(r, s, first):
                pe.wait_ge(S["gl_ready"], upto(r, s, M))
                for h in range(2):
                    for m in range(first, M):
                        a = mlp2_part(s, m, (2 * h, 2 * h + 1))
                        if h == 1 and m < M - 1:
                            a.then_inc(S["mlp2_done"], 1)
                    a.then_inc(S["ff_done"], 1)

            def slot(j):
                r = j.r
                before = Slot(r, j.s - 1, rounds)

                def first_half(*ms):
                    if j.mlp is not None:
                        for m in ms:
                            mlp1(r, j.mlp, m)

                def second_half(m):
                    if j.mlp is not None:
                        mlp2(r, j.mlp, m)

                def side_read():
                    if before.gat_wh is not None and not before.tail:
                        pe.wait_ge(S["wh_ready"], upto_gat(r, before.gat_wh, 2))
                    elif before.gat_soft is not None:
                        pe.wait_ge(S["gscores_sum"], upto_gat(r, before.gat_soft))
                        pe.wait_ge(S["ga_ready"], upto_gat(r, before.gat_soft))
                    elif before.score is not None:
                        pe.wait_ge(S["scores_sum"], upto(r, before.score))

                def side_read_again():
                    if j.gat_out is not None and not j.tail:
                        pe.wait_ge(S["gmix_leaky"], upto_gat(r, j.gat_out, 2))
                    elif j.mix is None:
                        side_read()

                def ut_turn():
                    if j.gat_wh is None:
                        return
                    b = buf_of(j.gat_wh)
                    pe.wait_ge(normed["u"], upto_gat(r, j.gat_wh))
                    if before.mix is not None:
                        pe.wait_ge(S["ht_ready"], upto(r, before.mix, KD))
                    elif before.tail and before.gat_wh is not None:
                        pe.wait_ge(S["wh_ready"], upto_gat(r, before.gat_wh, 2))
                    elif before.gat_wh is not None:
                        pe.wait_ge(S["ut_ready"], upto_gat(r, before.gat_wh, KD))
                    for k in range(KD):
                        for t in range(T):
                            a = pe.transpose(big_k[:, k, t * P:(t + 1) * P], u[:, b, t, k * P:(k + 1) * P], ident[:])
                        a.then_inc(S["ut_turned"], 1)

                def gat_mixing():
                    if j.gat_out is None:
                        return
                    pe.wait_ge(S["gprobs"], upto_gat(r, j.gat_out))
                    if j.tail:
                        pe.wait_ge(S["ff_added"], upto(r, ROUND - 1, 2))
                        if before.gat_out is not None:
                            pe.wait_ge(S["gmix_leaky"], upto_gat(r, before.gat_out, 2))
                    elif j.mix is None:
                        side_read()
                    w = wh[:, buf_of(j.gat_out) % 2]
                    g = gat_scores(j, j.gat_out)
                    for t in range(T):
                        a = pe.matmul(gat_mix(j)[:, t], g[:, t], w[:, t], start=True, stop=True)
                        if t % 2:
                            a.then_inc(S["gmix_done"], 1)

                def mask_turn():
                    if j.gat_soft is None:
                        return
                    side_read_again()
                    pe.wait_ge(S["m01_ready"], upto_gat(r, j.gat_soft, per_tile))
                    for t in range(T):
                        a = pe.transpose(turn_b[:, t], m01[:, t], ident_b[:])
                    a.then_inc(S["masks_turned"], 1)

                def gat_spread():
                    if j.gat_soft is None:
                        return
                    pe.wait_ge(S["gscores_in"], upto_gat(r, j.gat_soft, 2))
                    if j.score is not None:
                        pe.wait_ge(S["scores_sum"], upto(r, j.score))
                    for t in range(T):
                        a = pe.transpose(spread[:, t], gsc[:, t:t + 1].broadcast_to([P, P]), ident[:])
                    a.then_inc(S["gspread_done"], 1)

                def wu():
                    if j.gat_wh is None:
                        return
                    pe.wait_ge(S["ut_ready"], upto_gat(r, j.gat_wh, KD))
                    if j.tail:
                        pass
                    elif j.gat_soft is not None:
                        pe.wait_ge(S["gscores_sum"], upto_gat(r, j.gat_soft))
                        pe.wait_ge(S["ga_ready"], upto_gat(r, j.gat_soft))
                    elif j.score is not None:
                        pe.wait_ge(S["scores_sum"], upto(r, j.score))
                    else:
                        side_read_again()
                    for t in range(T):
                        for k in range(KD):
                            a = pe.matmul(wh_banks(j)[:, t], ut[:, k, t * P:(t + 1) * P], gw[:, k], start=(k == 0),
                                          stop=(k == KD - 1))
                        if t % 2:
                            a.then_inc(S["wh_done"], 1)

                if j.tail:
                    ut_turn()
                    mask_turn()
                    gat_spread()
                    gat_mixing()
                    wu()
                    return
                if isinstance(r, int) and r == 0 and j.s == 0:
                    pe.wait_ge(S["gw_in"], 32)
                first_half(1)
                ut_turn()
                first_half(2)
                if j.mix is not None:
                    pe.wait_ge(S["exp_done"], upto(r, j.mix))
                    side_read()
                    for t in range(T):
                        a = pe.transpose(turn[:, t], sp[:, t], ident[:])
                    a.then_inc(S["probs_turned"], 1)
                second_half(0)
                first_half(3)
                if j.mix is not None:
                    b = buf_of(j.mix)
                    pe.wait_ge(S["probs_ready"], upto(r, j.mix))
                    if j.gat_wh is not None:
                        pe.wait_ge(S["ut_ready"], upto_gat(r, j.gat_wh, KD))
                    elif before.mix is not None:
                        pe.wait_ge(S["ht_ready"], upto(r, before.mix, KD))
                    for t in range(T):
                        a = pe.matmul(big_t[:, t], pt[:, t], xb[:, b, t], start=True, stop=True)
                        if t % 2:
                            a.then_inc(S["mix_done"], 1)
                gat_mixing()
                first_half(4)
                second_half(1)
                first_half(5)
                second_half(2)
                first_half(6)
                if j.mix is not None:
                    b = buf_of(j.mix)
                    pe.wait_ge(normed["mix"], upto(r, j.mix))
                    for k in range(KD):
                        for t in range(T):
                            a = pe.transpose(big_k[:, k, t * P:(t + 1) * P], xb[:, b, t, k * P:(k + 1) * P], ident[:])
                        a.then_inc(S["z_turned"], 1)
                second_half(3)
                if j.score is not None:
                    pe.wait_ge(S["scores_in"], upto(r, j.score, 2))
                    side_read_again()
                    for t in range(T):
                        a = pe.transpose(spread[:, t], sc[:, j.score % 2, T + t:T + t + 1].broadcast_to([P, P]),
                                         ident[:])
                    a.then_inc(S["spread_done"], 1)
                mask_turn()
                first_half(7)
                second_half(4)
                gat_spread()
                second_half(5)
                if j.mix is not None:
                    mlp1(r, j.mix, 0)
                wu()
                if j.mlp is not None:
                    mlp2_last(r, j.mlp, 6)

            slots_of(pe, slot)

        @block.vector
        def _(dve):
            dve.wait_ge(S["cols_turned"], 1)
            dve.tensor_copy(cols[:], turn[:, 0, 0:NCOL]).then_inc(S["cols_ready"], 1)
            dve.wait_ge(S["ident_ready"], 2)
            dve.tensor_copy(ident_b[:], ident[:]).then_inc(S["cols_ready"], 1)
            for a in range(per_tile):
                i = slice(a * nodes, (a + 1) * nodes)
                dve.tensor_copy(eye[i, :], ident[i, i]).then_inc(S["cols_ready"], 1)
            dve.wait_ge(S["cols_ready"], 2 + per_tile)
            dve.wait_ge(S["mask_ready0"], 2)
            dve.wait_ge(S["consts_ready"], 2)
            for a in range(per_tile):
                i = slice(a * nodes, (a + 1) * nodes)
                dve.memset(gat_off[i, i], GAT_OFF).then_inc(S["consts_ready"], 1)
            dve.wait_ge(S["rows_in"], 32)

            def wait_alone(s, count):
                dve.wait_ge(S["cols_ready"], 2)
                dve.wait_ge(s, count)

            def split_weight(w):
                l = w // 2
                hi, lo = ((w1h, w1l) if w % 2 == 0 else (w2h, w2l))
                dve.wait_ge(w_in[w % 2], 16 * (w // 2 + 1))
                dve.tensor_copy(hi[:, l], stage_view(w)).then_inc(S["split_hi"], 1)
                dve.wait_ge(S["split_hi"], w + 1)
                dve.tensor_tensor(lo[:, l], stage_view(w), hi[:, l].bitcast(F32), ALU.subtract).then_inc(
                    S["split_lo"], 1)

            def statistics(name, y, count, wait_tile):
                for t in range(T):
                    wait_tile(t)
                    a = dve.bn_stats(st[name][:, t], y[:, t])
                a.then_inc(stats_done[name], 1)
                wait_alone(stats_done[name], count)
                for t in range(T):
                    a = dve.bn_aggr(mv[name][:, t], st[name][:, t])
                a.then_inc(mean_done[name], 1)
                dve.wait_ge(mean_done[name], count)
                if name in nmean:
                    dve.tensor_scalar(nmean[name][:], mv[name][:, :, 0], -1.0, None, ALU.mult)
                dve.tensor_scalar(ve[name][:], mv[name][:, :, 1], EPS, None, ALU.add).then_inc(var_ready[name], 1)

            def normalise(name, y, count):
                dve.wait_ge(dev_ready[name], count)
                for t in range(T):
                    a = dve.tensor_scalar(y[:, t], y[:, t], mv[name][:, t, 0:1], rd[name][:, t:t + 1],
                                          ALU.subtract, ALU.mult)
                a.then_inc(normed[name], 1)

            def pair_scores(src, w_row, dst, bias, done, first_done, parts=(0, 1)):
                for c in parts:
                    if c == 1:
                        dve.wait_ge(done, first_done)
                    for t in range(T):
                        a = dve.tensor_tensor_reduce(unread[:, t], src[:, t], w_row[:, c * D:(c + 1) * D], 1.0,
                                                     bias if c == 0 else 0.0, ALU.mult, ALU.add,
                                                     dst[:, c * T + t:c * T + t + 1])
                    a.then_inc(done, 1)

            def slot(j):
                r = j.r

                def gl_part(*ms):
                    if j.mlp is not None:
                        for m in ms:
                            dve.wait_ge(S["gelu_done"], upto(r, j.mlp, M, m + 1))
                            wait_room(dve, r, j.mlp, m)
                            dve.tensor_tensor(gl[:, m % 4], gt[:, m % 2], gh[:, m % 4].bitcast(F32),
                                              ALU.subtract).then_inc(S["gl_ready"], 1)

                def next_pair_scores(*parts):
                    if j.pair is None:
                        return
                    b, l = buf_of(j.pair), layer_of(j.pair)
                    if isinstance(r, int) and r == 0 and j.pair == BUFS:
                        dve.wait_ge(S["more_rows_in"], 16)
                    if 0 in parts:
                        if l == 0:
                            dve.wait_ge(x_in[b], r * 16 + 16 * (j.pair // ROUND + 1))
                        else:
                            dve.wait_ge(S["x_ready"], upto(r, j.pair - BUFS))
                        before = Slot(r, j.s - 1, rounds)
                        if before.score is not None:
                            dve.wait_ge(S["scores_sum"], upto(r, before.score))
                        if before.gat_wh is not None:
                            dve.wait_ge(S["gscores_in"], upto_gat(r, before.gat_wh, 2))
                    pair_scores(xb[:, b], score_w[:, l], sc[:, j.pair % 2], score_b[:, l:l + 1], S["scores_in"],
                                upto(r, j.pair, 2, 1), parts)

                def split_in(*slots):
                    if isinstance(r, int) and r == 0 and j.s in slots:
                        split_weight(j.s + 2)

                def mlp_sum(h):
                    if j.norm is None:
                        return
                    if h == 0:
                        dve.wait_ge(S["h_ready"], upto(r, j.norm))
                    y = xb[:, buf_of(j.norm), 2 * h:2 * h + 2]
                    dve.wait_ge(S["ff_done"], upto(r, j.norm, 2, h + 1))
                    dve.tensor_tensor(y, ff[:, 2 * h:2 * h + 2], y, ALU.add).then_inc(S["ff_added"], 1)

                def mlp_statistics():
                    if j.norm is None:
                        return
                    statistics("mlp", xb[:, buf_of(j.norm)], upto(r, j.norm),
                               lambda t: dve.wait_ge(S["ff_added"], upto(r, j.norm, 2, t // 2 + 1)))

                def gat_sum_inverse(job):
                    if job is None:
                        return
                    dve.wait_ge(S["gexp_done"], upto_gat(r, job))
                    dve.reciprocal(gri[:], grs[:]).then_inc(S["gsum_inverse"], 1)

                def u_statistics():
                    if j.gat_stats is None:
                        return
                    dve.wait_ge(S["u_added"], upto_gat(r, j.gat_stats))
                    statistics("u", u[:, buf_of(j.gat_stats)], upto_gat(r, j.gat_stats), lambda t: None)

                def mlp_norm():
                    if j.norm is None:
                        return
                    normalise("mlp", xb[:, buf_of(j.norm)], upto(r, j.norm))

                def gat_leaky():
                    if j.gat_out is None:
                        return
                    for h in range(2):
                        dve.wait_ge(S["gmix_scaled"], upto_gat(r, j.gat_out, 2, h + 1))
                        w = mix_room(j)[:, 2 * h:2 * h + 2]
                        dve.tensor_tensor(w, gat_mix(j)[:, 2 * h:2 * h + 2], w, ALU.max).then_inc(S["gmix_leaky"], 1)

                def out_statistics():
                    if j.gat_out is None:
                        return
                    dve.wait_ge(S["out_added"], upto_gat(r, j.gat_out))
                    statistics("out", u[:, buf_of(j.gat_out)], upto_gat(r, j.gat_out), lambda t: None)

                def gat_masks():
                    if j.gat_soft is None:
                        return
                    dve.wait_ge(S["masks_turned"], upto_gat(r, j.gat_soft))
                    dve.tensor_copy(gm[:, :, :], turn_b).then_inc(S["gm_ready"], 1)
                    dve.scalar_tensor_tensor(
                        out=ga[:, :, :], in0=turn_b, scalar=-GAT_OFF,
                        in1=gat_off[:].rearrange("p (o n) -> p o n", o=1).broadcast_to([P, T, P]),
                        op0=ALU.mult, op1=ALU.add).then_inc(S["ga_ready"], 1)
                    dve.wait_ge(S["gscores_sum"], upto_gat(r, j.gat_soft))
                    g = gat_scores(j, j.gat_soft)
                    dve.scalar_tensor_tensor(out=g[:, :, :], in0=g[:, :, :], scalar=SLOPE, in1=g[:, :, :],
                                             op0=ALU.mult, op1=ALU.max).then_inc(S["gleaky"], 1)

                def gat_max():
                    if j.gat_soft is None:
                        return
                    wait_alone(S["gmasked"], upto_gat(r, j.gat_soft))
                    dve.wait_ge(S["ga_ready"], upto_gat(r, j.gat_soft))
                    g = gat_scores(j, j.gat_soft)
                    for t in range(T):
                        a = dve.tensor_tensor_reduce(g[:, t], g[:, t], ga[:, t], 1.0, OFF, ALU.add, ALU.max,
                                                     gmx[:, t:t + 1])
                    a.then_inc(S["gmax_done"], 1)
                    dve.wait_ge(S["gmax_done"], upto_gat(r, j.gat_soft))
                    dve.tensor_scalar(gnm[:], gmx[:], -1.0, None, ALU.mult).then_inc(S["gnegmax"], 1)

                def edges():
                    if j.gat_wh is None:
                        return
                    dve.wait_ge(S["adj_t_in"], upto_gat(r, j.gat_wh, 16))
                    if j.gat_soft is not None:
                        dve.wait_ge(S["gmasked"], upto_gat(r, j.gat_soft))
                    for a in range(per_tile):
                        i = slice(a * nodes, (a + 1) * nodes)
                        dve.tensor_scalar(m01[i, :, i], adj_t[i], 0.0, None, ALU.is_gt).then_inc(S["m01_ready"], 1)

                def wh_scores(job, pair):
                    if job is None:
                        return
                    w = wh[:, buf_of(job) % 2]
                    dve.wait_ge(S["wh_ready"], upto_gat(r, job, 2))
                    if pair is not None:
                        dve.wait_ge(S["scores_in"], upto(r, pair, 2))
                    pair_scores(w, gat_w[:], gsc, 0.0, S["gscores_in"], upto_gat(r, job, 2, 1))

                before = Slot(r, j.s - 1, rounds)

                if j.tail:
                    mlp_sum(0)
                    mlp_sum(1)
                    if not before.tail:
                        wh_scores(before.gat_wh, before.pair)
                    mlp_statistics()
                    gat_masks()
                    gat_leaky()
                    u_statistics()
                    mlp_norm()
                    gat_max()
                    edges()
                    wh_scores(j.gat_wh, None)
                    gat_sum_inverse(j.gat_soft)
                    out_statistics()
                    return
                split_in(-2)
                mlp_sum(0)
                gl_part(0)
                mlp_sum(1)
                mlp_statistics()
                if j.mix is not None:
                    dve.wait_ge(S["exp_done"], upto(r, j.mix))
                    dve.reciprocal(ri[:], rs[:]).then_inc(S["sum_inverse"], 1)
                gat_sum_inverse(j.gat_out)
                wh_scores(before.gat_wh, before.pair)
                gl_part(1)
                mlp_norm()
                if j.mix is not None:
                    b = buf_of(j.mix)
                    dve.wait_ge(S["sum_inverse"], upto(r, j.mix))
                    for t in range(T):
                        if t % 2 == 0:
                            dve.wait_ge(S["mix_done"], upto(r, j.mix, 2, t // 2 + 1))
                        dve.scalar_tensor_tensor(out=xb[:, b, t], in0=big_t[:, t], scalar=ri[:, t:t + 1],
                                                 in1=xb[:, b, t], op0=ALU.mult, op1=ALU.add).then_inc(
                                                     S["mix_added"], 1)
                gl_part(2)
                if j.mix is not None:
                    statistics("mix", xb[:, buf_of(j.mix)], upto(r, j.mix),
                               lambda t: dve.wait_ge(S["mix_added"], upto(r, j.mix, T, t + 1)))
                gl_part(3)
                if j.mix is not None:
                    normalise("mix", xb[:, buf_of(j.mix)], upto(r, j.mix))
                gat_leaky()
                gl_part(4, 5)
                u_statistics()
                split_in(-1)
                out_statistics()
                early = j.fresh is None and j.gat_soft is None and j.gat_out is None
                if early:
                    next_pair_scores(0)
                if j.score is not None:
                    b = buf_of(j.score)
                    if layer_of(j.score) == 0:
                        dve.wait_ge(S["mask_ready"], upto_gat(r, j.score, per_tile))
                    dve.wait_ge(S["scores_sum"], upto(r, j.score))
                    dve.scalar_tensor_tensor(out=sp[:, :, :], in0=sp[:, :, :], scalar=SLOPE, in1=sp[:, :, :],
                                             op0=ALU.mult, op1=ALU.max).then_inc(S["scores_leaky"], 1)
                    wait_alone(S["scores_leaky"], upto(r, j.score))
                    for t in range(T):
                        a = dve.tensor_tensor_reduce(sp[:, t], sp[:, t], mask[:, b, t], 1.0, OFF, ALU.add, ALU.max,
                                                     mx[:, t:t + 1])
                    a.then_inc(S["max_done"], 1)
                    dve.wait_ge(S["max_done"], upto(r, j.score))
                    dve.tensor_scalar(nm[:], mx[:], -1.0, None, ALU.mult).then_inc(S["negmax"], 1)
                gat_masks()
                gl_part(6)
                gl_part(7)
                gat_max()
                if j.fresh is not None:
                    b = buf_of(j.fresh)
                    dve.wait_ge(S["adj_a_in"], upto_gat(r, j.fresh, 16))
                    dve.tensor_tensor(adj_e[:], adj_a[:], eye[:].rearrange("p (o j) -> p o j", o=1).broadcast_to(
                        [P, T, nodes]), ALU.add).then_inc(S["mask_edges"], 1)
                    dve.wait_ge(S["mask_edges"], upto_gat(r, j.fresh))
                    for a in range(per_tile):
                        i = slice(a * nodes, (a + 1) * nodes)
                        dve.tensor_scalar(mask[i, b, :, i], adj_e[i], 0.0, OFF, ALU.is_le, ALU.mult).then_inc(
                            S["mask_ready"], 1)
                edges()
                next_pair_scores(*((1,) if early else (0, 1)))
                split_in(*range(0, N_SPLITS - 2))

            slots_of(dve, slot)


_INS = ['x', 'adj', 'L0_gnn_attn_w', 'L0_gnn_attn_b', 'L0_gnn_W1', 'L0_gnn_b1', 'L0_gnn_W2', 'L0_gnn_b2',
        'L0_gnn_g1', 'L0_gnn_beta1', 'L0_gnn_g2', 'L0_gnn_beta2', 'L1_gnn_W', 'L1_gnn_a']


def kernel(**inputs):
    import numpy as _np
    import concourse.bacc as _bacc
    from concourse import mybir as _mybir
    from concourse.bass_utils import run_bass_kernel_spmd as _run

    nc = _bacc.Bacc("TRN2", target_bir_lowering=False, num_devices=1, dynamic_dma_scratch_size=1024)
    arrays, args = {}, []
    for name in _INS:
        a = _np.ascontiguousarray(inputs[name])
        arrays[f"in_{name}_dram"] = a
        args.append(nc.dram_tensor(f"in_{name}_dram", a.shape, _mybir.dt.from_np(a.dtype), kind="ExternalInput").ap())
    shape = tuple(inputs['x'].shape)
    args.append(nc.dram_tensor("out_0_dram", shape, _mybir.dt.float32, kind="ExternalOutput").ap())
    graph_net_kernel(nc, *args)
    r = _run(nc, [arrays], core_ids=[0])
    return r.results[0]["out_0_dram"]
```
